# Optimizing a Trainium2 kernel written in Bass

```python
import numpy as np
import jax
import jax.numpy as jnp

def _softmax(x, axis=-1):
    return jax.nn.softmax(x, axis=axis)

def _gelu(x):
    return jax.nn.gelu(x, approximate=True)

def _silu(x):
    return jax.nn.silu(x)

def _sigmoid(x):
    return jax.nn.sigmoid(x)

def _layernorm(x, axis=-1, eps=1e-05):
    m = jnp.mean(x, axis=axis, keepdims=True)
    v = jnp.var(x, axis=axis, keepdims=True)
    return (x - m) / jnp.sqrt(v + eps)

def _scatter_add(tgt, idx, src, axis=0):
    return tgt.at[idx].add(src)

def _segment_sum(src, seg, n):
    return jax.ops.segment_sum(src, seg, n)
kernel_name = 'mk_gnn_resnorm_d1_gnn_r8_99b27d'

def setup_inputs(seed: int=0):
    np.random.seed(seed)
    _w = jnp.asarray

    def _rec_inputs():
        import jax
        import jax.numpy as jnp
        _gk = jax.random.key(seed)
        x = -0.0003713 + 1 * jax.random.normal(jax.random.fold_in(_gk, 1), (6250, 128), jnp.float32)
        _s = jax.random.randint(jax.random.fold_in(_gk, 2), (100000,), 0, 6250, jnp.int32)
        _d = jax.random.randint(jax.random.fold_in(_gk, 3), (100000,), 0, 6250, jnp.int32)
        _loop = jnp.arange(6250, dtype=jnp.int32)
        src = jnp.concatenate([_s, _d, _loop])
        dst = jnp.concatenate([_d, _s, _loop])
        _o = jnp.argsort(dst, stable=True)
        src = src[_o]
        dst = dst[_o]
        edge_attr_128 = 5.93493e-05 + 1.00006 * jax.random.normal(jax.random.fold_in(_gk, 11), (206250, 128), jnp.float32)
        return (x, src, dst, edge_attr_128)
    x, src, dst, edge_attr_128 = _rec_inputs()

    def _L0_gnn_setup():
        import jax, jax.numpy as jnp
        import numpy as np
        N_NODES = 12500
        N_EDGES = 75000
        HIDDEN = 128
        key = jax.random.key(seed)
        ks = jax.random.split(key, 12)
        s = 0.05
        x = jax.random.normal(ks[0], (N_NODES, HIDDEN), dtype=jnp.float32)
        edge_index = jax.random.randint(ks[1], (2, N_EDGES), 0, N_NODES, dtype=jnp.int64)
        edge_features = jax.random.normal(ks[2], (N_EDGES, HIDDEN), dtype=jnp.float32)
        global_feat = jax.random.normal(ks[3], (1, HIDDEN), dtype=jnp.float32)
        W_c = jax.random.normal(ks[4], (3 * HIDDEN, HIDDEN), dtype=jnp.float32) * s
        b_c = jnp.zeros((HIDDEN,), dtype=jnp.float32)
        W1 = jax.random.normal(ks[5], (HIDDEN, HIDDEN), dtype=jnp.float32) * s
        b1 = jnp.zeros((HIDDEN,), dtype=jnp.float32)
        W2 = jax.random.normal(ks[6], (HIDDEN, HIDDEN), dtype=jnp.float32) * s
        b2 = jnp.zeros((HIDDEN,), dtype=jnp.float32)
        W3 = jax.random.normal(ks[7], (HIDDEN, HIDDEN), dtype=jnp.float32) * s
        b3 = jnp.zeros((HIDDEN,), dtype=jnp.float32)
        return {'x': x, 'edge_index': edge_index, 'edge_features': edge_features, 'global_feat': global_feat, 'W_c': W_c, 'b_c': b_c, 'W1': W1, 'b1': b1, 'W2': W2, 'b2': b2, 'W3': W3, 'b3': b3}
    _L0_gnn_all = _L0_gnn_setup()
    _L0_gnn_in = {k: v for k, v in _L0_gnn_all.items() if k in ('global_feat', 'W_c', 'b_c', 'W1', 'b1', 'W2', 'b2', 'W3', 'b3')}
    del _L0_gnn_all
    return {'x': x, 'src': src, 'dst': dst, 'edge_attr_128': edge_attr_128, 'L0_gnn_global_feat': _L0_gnn_in['global_feat'], 'L0_gnn_W_c': _L0_gnn_in['W_c'], 'L0_gnn_b_c': _L0_gnn_in['b_c'], 'L0_gnn_W1': _L0_gnn_in['W1'], 'L0_gnn_b1': _L0_gnn_in['b1'], 'L0_gnn_W2': _L0_gnn_in['W2'], 'L0_gnn_b2': _L0_gnn_in['b2'], 'L0_gnn_W3': _L0_gnn_in['W3'], 'L0_gnn_b3': _L0_gnn_in['b3']}

def reference(x, src, dst, edge_attr_128, L0_gnn_global_feat, L0_gnn_W_c, L0_gnn_b_c, L0_gnn_W1, L0_gnn_b1, L0_gnn_W2, L0_gnn_b2, L0_gnn_W3, L0_gnn_b3):
    import jax
    import jax.numpy as jnp

    def _L0_gnn_ref(x, edge_index, edge_features, global_feat, W_c, b_c, W1, b1, W2, b2, W3, b3):
        import jax, jax.numpy as jnp
        import numpy as np
        N_NODES = 12500
        N_EDGES = 75000
        HIDDEN = 128
        n = x.shape[0]
        row = edge_index[0]
        edge_aggr = jnp.zeros((n, HIDDEN), dtype=x.dtype).at[row].add(edge_features)
        reps = n // global_feat.shape[0]
        global_expand = jnp.repeat(global_feat, reps, axis=0)
        combined = jnp.concatenate([x, edge_aggr, global_expand], axis=-1) @ W_c + b_c
        h = jax.nn.softplus(combined @ W1 + b1)
        h = jax.nn.softplus(h @ W2 + b2)
        return h @ W3 + b3
    edge_index = jnp.stack([src, dst])
    x = _layernorm(x + _L0_gnn_ref(x, edge_index, edge_attr_128, L0_gnn_global_feat, L0_gnn_W_c, L0_gnn_b_c, L0_gnn_W1, L0_gnn_b1, L0_gnn_W2, L0_gnn_b2, L0_gnn_W3, L0_gnn_b3), axis=-1)
    return x

_drawn_inputs = setup_inputs


def setup_inputs(seed=0):
    import zlib

    import numpy as np

    out = dict(_drawn_inputs(seed))
    spreads = {'L0_gnn_b_c': (0.0, 0.8),
     'L0_gnn_b1': (0.0, 0.8),
     'L0_gnn_b2': (0.0, 0.303),
     'L0_gnn_b3': (0.0, 0.1)}
    factors = {}
    for name, (base, spread) in spreads.items():
        noise = np.random.default_rng([zlib.crc32(name.encode()), seed]).standard_normal(out[name].shape)
        drawn = base * np.exp(spread * noise) if base else spread * noise
        out[name] = jnp.asarray(drawn.astype(out[name].dtype))
    for name, factor in factors.items():
        out[name] = (out[name] * factor).astype(out[name].dtype)
    return out
```

```python
import concourse.bass as bass
from concourse import mybir
from contextlib import ExitStack


def gnn_edge_sum_mlp_layernorm(nc, x, xT, src, feats, glob, W_c, b_c, W1, b1, W2, b2, W3, b3, out):
    fp32, bf16, i32 = mybir.dt.float32, mybir.dt.bfloat16, mybir.dt.int32
    ALU = mybir.AluOpType
    ACT = mybir.ActivationFunctionType

    P = 128
    N, D = x.shape
    E = src.shape[0]
    COLS = E // P
    REST = E - COLS * P
    TILES = COLS + 1
    QUAD = 4
    GROUP = 16
    QG = GROUP // QUAD
    SLOTS = 2
    PADDED = -(-TILES // GROUP) * GROUP
    BODIES = TILES // (SLOTS * GROUP)
    LEFT = TILES - BODIES * SLOTS * GROUP
    LAST = BODIES * SLOTS
    TABLES = 4
    PER = GROUP // TABLES
    NP_ = 125
    NT = N // NP_
    ROWS = P * NT
    assert NP_ * NT == N and ROWS >= N + P and 0 < LEFT <= GROUP and LEFT % QUAD == 0
    EPS = 1e-5

    feats_v = feats[0:COLS * P, :].rearrange("(p t) f -> p (t f)", t=COLS)
    src_v = src[0:COLS * P].rearrange("(p t) -> p t", t=COLS)
    tables = [nc.dram_tensor(f"node_table{k}", (ROWS, D), fp32, kind="Internal").ap() for k in range(TABLES)]
    tables_v = [t.rearrange("(p t) f -> p (t f)", t=NT) for t in tables]
    out_v = out.rearrange("(p t) f -> p (t f)", t=NT)

    ctx = ExitStack()
    with ctx:
        def sb(name, shape, dt=fp32):
            return ctx.enter_context(nc.sbuf_tensor(name, shape, dt))

        def sem(name):
            return ctx.enter_context(nc.semaphore(name))

        ids_i = sb("ids_i", [P, PADDED], i32)
        ids_f = sb("ids_f", [P, PADDED])
        ids_hi = sb("ids_hi", [P, PADDED], bf16)
        ids_lo = sb("ids_lo", [P, PADDED], bf16)
        to_spare = sb("to_spare", [P, PADDED])
        ids_now = sb("ids_now", [P, SLOTS, 2, GROUP], bf16)
        col_now = sb("col_now", [P, SLOTS, GROUP])
        feat = sb("feat", [P, SLOTS, GROUP * D])
        same = sb("same", [P, 2, QUAD * P])
        rows = sb("rows", [P, SLOTS, GROUP * D])
        moved = sb("moved", [P, SLOTS, GROUP])
        index = sb("index", [P, SLOTS, GROUP], i32)
        zeros = sb("zeros", [P, 10 * D])
        ident = sb("ident", [P, P])
        ident16 = sb("ident16", [P, P], bf16)
        spare_i = sb("spare_i", [P, 1], i32)
        spare_f = sb("spare_f", [P, 1])
        power_i = sb("power_i", [P, 1], i32)
        power = power_i[:, :].bitcast(fp32)
        limit = sb("limit", [P, 1])
        wc = sb("wc", [P, 3, D])
        w1 = sb("w1", [P, D])
        w2 = sb("w2", [P, D])
        w3 = sb("w3", [P, D])
        wcT = sb("wcT", [P, 2, D])
        wxa = sb("wxa", [P, 2, D])
        col_glob = sb("col_glob", [P, 1])
        col_bc = sb("col_bc", [P, 1])
        col_b1 = sb("col_b1", [P, 1])
        col_b2 = sb("col_b2", [P, 1])
        const_c = sb("const_c", [P, 1])
        const_1 = sb("const_1", [P, 1])
        b3row = sb("b3row", [1, D])
        b3all = sb("b3all", [P, D])
        ones = sb("ones", [1, P])
        eps = sb("eps", [P, 1])
        xn = sb("xn", [NP_, NT * D])
        xt = sb("xt", [P, NT * NP_])
        CH = 4
        chunks = [(c, min(CH, NT - c)) for c in range(0, NT, CH)]
        NCH = len(chunks)
        aggT = sb("aggT", [P, 2, CH * NP_])
        act_a = sb("act_a", [P, 2, 2, CH * NP_])
        act_z = sb("act_z", [P, 2, 2, CH * NP_])
        act_h = sb("act_h", [P, 2, 2, CH * NP_])
        stats = sb("stats", [P, 2, CH, 6])
        mv = sb("mv", [P, 2, CH, 2])
        var = sb("var", [P, 2, CH])
        logv = sb("logv", [P, 2, CH])
        guess = sb("guess", [P, 2, CH])
        newt = sb("newt", [P, 2, 3, CH])
        assert TABLES * CH * D == GROUP * D and 2 * CH * D * 2 == GROUP * D
        tab = rows[:, :, :].rearrange("p s (k n) -> p s k n", k=TABLES)
        half = feat[:, 0, :].rearrange("p (s h n) -> p s h n", s=2, h=2)

        ps = ctx.enter_context(nc.psum_tensor("ps", [P, 8, 512], fp32))
        SPREAD, SUMS, COUNTS = 0, 2, 4
        TURN, LIN1, LIN2, LIN3 = 0, 2, 4, 6

        zeros_set = sem("zeros_set")
        ones_set = sem("ones_set")
        pads_set = sem("pads_set")
        consts_a = sem("consts_a")
        consts_set = sem("consts_set")
        spare_set = sem("spare_set")
        ident_cast = sem("ident_cast")
        ids_loaded = sem("ids_loaded")
        ids_cast = sem("ids_cast")
        ids_split = sem("ids_split")
        ids_staged = sem("ids_staged")
        rest_zeroed = sem("rest_zeroed")
        ids_spread = sem("ids_spread")
        same_ready = sem("same_ready")
        summed = sem("summed")
        rows_ready = sem("rows_ready")
        moved_ready = sem("moved_ready")
        index_ready = sem("index_ready")
        weights_loaded = sem("weights_loaded")
        x_loaded = sem("x_loaded")
        turned_w = sem("turned_w")
        turned_w_copied = sem("turned_w_copied")
        const_c_done = sem("const_c_done")
        const_c_ready = sem("const_c_ready")
        folded = sem("folded")
        folded_ready = sem("folded_ready")
        const_1_done = sem("const_1_done")
        const_1_ready = sem("const_1_ready")
        b3_spread = sem("b3_spread")
        b3_ready = sem("b3_ready")
        xb_ready = sem("xb_ready")
        half_a = sem("half_a")
        half_b = sem("half_b")
        turned = sem("turned")
        aggT_ready = sem("aggT_ready")
        lin3_done = sem("lin3_done")
        resid_done = sem("resid_done")
        stats_done = sem("stats_done")
        aggr_done = sem("aggr_done")
        var_ready = sem("var_ready")
        logv_done = sem("logv_done")
        guess_ready = sem("guess_ready")
        newt_a = sem("newt_a")
        newt_b = sem("newt_b")
        newt_c = sem("newt_c")
        rstd_ready = sem("rstd_ready")
        normed = sem("normed")
        out_sent = sem("out_sent")
        feats_loaded = [sem(f"feats_loaded{s}") for s in range(SLOTS)]
        tables_zeroed = [sem(f"table_zeroed{k}") for k in range(TABLES)]
        table_settled = [sem(f"table_settled{k}") for k in range(TABLES)]
        tab_loaded = [sem(f"tab_loaded{s}") for s in range(2)]
        lin_done = [sem(f"lin{n}_done") for n in (1, 2)]
        abs_done = [sem(f"abs{n}_done") for n in (1, 2)]
        exp_done = [sem(f"exp{n}_done") for n in (1, 2)]
        log_done = [sem(f"log{n}_done") for n in (1, 2)]
        z_ready = [sem(f"z{n}_ready") for n in (1, 2)]
        hidden = [sem(f"hidden{n}_ready") for n in (1, 2)]

        def wait(eng, s, value):
            if not isinstance(value, int) or value > 0:
                eng.wait_ge(s, value)

        def over_groups(eng, do):
            for s in range(SLOTS):
                do(0, s, QG)
            with eng.Fori(1, BODIES) as i:
                for s in range(SLOTS):
                    do(i, s, QG)
            do(BODIES, 0, LEFT // QUAD)

        def scattered_before(eng, i, s):
            if not isinstance(i, int) or i > 0:
                for k in range(TABLES):
                    eng.wait_ge(table_settled[k], (i * SLOTS + (s - SLOTS + 1)) * (16 * PER))

        def q_slot(s, q):
            return (s * QG + q) % 2

        block = ctx.enter_context(nc.Block())

        @block.sync
        def _(sp):
            sp.dma_start(ids_i[:, 0:COLS], src_v).then_inc(ids_loaded, 16)
            sp.wait_ge(pads_set, 1)
            sp.dma_start(ids_i[0:REST, COLS:TILES], src[COLS * P:E].rearrange("(p t) -> p t", t=1))\
              .then_inc(ids_loaded, 16)

            def load(i, s):
                sp.dma_start(feat[:, s, :], feats_v[:, bass.ds((i * SLOTS + s) * (GROUP * D), GROUP * D)])\
                  .then_inc(feats_loaded[s], 16)

            sp.wait_ge(zeros_set, 1)
            for k in range(TABLES):
                for j in range(0, NT, 10):
                    sp.dma_start(tables_v[k][:, j * D:(j + 10) * D], zeros[:, :])\
                      .then_inc(tables_zeroed[k], 16)
                if k < SLOTS:
                    load(0, k)
            sp.dma_start(xn[:, :], x.rearrange("(p t) f -> p (t f)", t=NT)).then_inc(x_loaded, 16)
            sp.dma_start(xt[:, :], xT).then_inc(x_loaded, 16)
            with sp.Fori(1, BODIES) as i:
                for s in range(SLOTS):
                    sp.wait_ge(summed, i * (SLOTS * QG) + (s + 1 - SLOTS) * QG)
                    load(i, s)
            sp.wait_ge(summed, (LAST + 1 - SLOTS) * QG)
            n = (LEFT - 1) * D
            sp.dma_start(feat[:, 0, 0:n], feats_v[:, LAST * GROUP * D:LAST * GROUP * D + n])\
              .then_inc(feats_loaded[0], 16)
            sp.wait_ge(rest_zeroed, 1)
            sp.dma_start(feat[0:REST, 0, n:n + D], feats[COLS * P:E, :]).then_inc(feats_loaded[0], 16)

            for k in range(TABLES):
                sp.wait_ge(table_settled[k], TILES // TABLES * 16)

            def store(c):
                t0, nt = chunks[c]
                sp.wait_ge(normed, c + 1)
                for a, b in ((0, 112), (112, NP_)):
                    sp.dma_start(out_v[a:b, t0 * D:(t0 + nt) * D], xn[a:b, t0 * D:(t0 + nt) * D])\
                      .then_inc(out_sent, 16)

            for c, (t0, nt) in enumerate(chunks):
                wait(sp, half_a, c - 1)
                wait(sp, half_b, c - 1)
                for k in range(TABLES):
                    sp.dma_start(tab[:, c % 2, k, 0:nt * D], tables_v[k][:, t0 * D:(t0 + nt) * D])\
                      .then_inc(tab_loaded[c % 2], 16)
                if c >= 6:
                    store(c - 6)
            for c in range(NCH - 6, NCH):
                store(c)
            sp.wait_ge(out_sent, 32 * NCH)

        @block.gpsimd
        def _(pool):
            pool.iota(ids_i[:, COLS:PADDED], [[0, PADDED - COLS]], base=N, channel_multiplier=1)\
                .then_inc(pads_set, 1)
            pool.iota(spare_i[:, :], [[0, 1]], base=N, channel_multiplier=1).then_inc(consts_a, 1)
            pool.iota(power_i[:, :], [[0, 1]], base=(127 + 60) << 23, channel_multiplier=-(1 << 23))\
                .then_inc(consts_a, 1)
            pool.memset(ident[:, :], 0.0).then_inc(consts_a, 1)
            pool.wait_ge(consts_a, 3)
            pool.affine_select(out=ident[:, :], in_=ident[:, :], compare_op=ALU.not_equal, fill=1.0, base=0,
                               pattern=[[-1, P]], channel_multiplier=1).then_inc(consts_set, 1)
            for k in range(TABLES):
                pool.wait_ge(tables_zeroed[k], 16 * (NT // 10))

            def scatter(i, s, quads):
                pool.wait_ge(index_ready, i * SLOTS + (s + 1))
                for q in range(quads):
                    pool.wait_ge(rows_ready, i * (SLOTS * QG) + (s * QG + q + 1))
                    for k in range(TABLES):
                        t = q * TABLES + k
                        wait(pool, table_settled[k], i * (SLOTS * PER * 16) + (s * PER + q) * 16)
                        pool.nop(nofuse=True)
                        pool.indirect_dma_start(
                            tables[k], bass.IndirectOffsetOnAxis(ap=index[:, s, t:t + 1], axis=0),
                            rows[:, s, t * D:(t + 1) * D], None, compute_op=ALU.add)\
                            .then_inc(table_settled[k], 16)
            over_groups(pool, scatter)

            for c, (t0, nt) in enumerate(chunks):
                pool.wait_ge(tab_loaded[c % 2], 16 * TABLES * (c // 2 + 1))
                wait(pool, turned, c - 1)
                pool.tensor_tensor(half[:, c % 2, 1, 0:nt * D], tab[:, c % 2, 2, 0:nt * D],
                                   tab[:, c % 2, 3, 0:nt * D], ALU.add).then_inc(half_b, 1)

        @block.vector
        def _(dve):
            dve.memset(zeros[:, :], 0.0).then_inc(zeros_set, 1)
            dve.memset(ones[:, :], 1.0).then_inc(ones_set, 1)
            dve.memset(eps[:, :], EPS).then_inc(ones_set, 1)
            dve.wait_ge(consts_a, 3)
            dve.tensor_copy(spare_f[:, :], spare_i[:, :]).then_inc(spare_set, 1)
            dve.tensor_scalar(limit[:, :], power, 2.5, None, ALU.mult).then_inc(spare_set, 1)
            dve.wait_ge(consts_set, 1)
            dve.tensor_copy(ident16[:, :], ident[:, :]).then_inc(ident_cast, 1)
            dve.wait_ge(ids_loaded, 32)
            dve.tensor_copy(ids_f[:, :], ids_i[:, :]).then_inc(ids_cast, 1)
            dve.wait_ge(ids_cast, 1)
            dve.tensor_copy(ids_hi[:, :], ids_f[:, :]).then_inc(ids_cast, 1)
            dve.wait_ge(spare_set, 2)
            dve.tensor_scalar(to_spare[:, :], ids_f[:, :], -1.0, spare_f[:, :], ALU.mult, ALU.add)\
               .then_inc(ids_split, 1)
            dve.wait_ge(ids_cast, 2)
            dve.tensor_tensor(ids_lo[:, :], ids_f[:, :], ids_hi[:, :], ALU.subtract).then_inc(ids_split, 1)
            dve.wait_ge(ids_split, 2)

            def stage(g, s):
                at = bass.ds(g * GROUP, GROUP)
                dve.tensor_copy(ids_now[:, s, 0, :], ids_hi[:, at]).then_inc(ids_staged, 1)
                dve.tensor_copy(ids_now[:, s, 1, :], ids_lo[:, at]).then_inc(ids_staged, 1)
                dve.tensor_copy(col_now[:, s, :], ids_f[:, at]).then_inc(ids_staged, 1)

            def mark(i, s, quads):
                first_quad = i * (SLOTS * QG) + s * QG
                dve.wait_ge(ids_staged, i * (SLOTS * 3) + (s + 1) * 3)
                if isinstance(i, int) and i == BODIES:
                    dve.wait_ge(summed, (LAST + 1 - SLOTS) * QG)
                    dve.memset(feat[:, s, (LEFT - 1) * D:LEFT * D], 0.0).then_inc(rest_zeroed, 1)
                for q in range(quads):
                    dve.wait_ge(ids_spread, first_quad + (q + 1))
                    dve.tensor_tensor(
                        same[:, q_slot(s, q), :].rearrange("p (t e) -> p t e", t=QUAD),
                        ps[:, SPREAD + q_slot(s, q), :].rearrange("p (t e) -> p t e", t=QUAD),
                        col_now[:, s, q * QUAD:(q + 1) * QUAD].unsqueeze(2).to_broadcast([P, QUAD, P]),
                        ALU.is_equal).then_inc(same_ready, 1)
                    if q == 0 and not (isinstance(i, int) and i == BODIES):
                        stage(i * SLOTS + (s + 1), 1 - s)
                n = quads * QUAD
                at = bass.ds((i * SLOTS + s) * GROUP, n)
                dve.wait_ge(summed, first_quad + quads)
                dve.scalar_tensor_tensor(moved[:, s, 0:n], ps[:, COUNTS, s * GROUP:s * GROUP + n], limit[:, :],
                                         to_spare[:, at], ALU.is_ge, ALU.mult).then_inc(moved_ready, 1)
                scattered_before(dve, i, s)
                dve.wait_ge(moved_ready, i * SLOTS + (s + 1))
                dve.tensor_tensor(index[:, s, 0:n], moved[:, s, 0:n], ids_f[:, at], ALU.add)\
                   .then_inc(index_ready, 1)

            stage(0, 0)
            over_groups(dve, mark)

            dve.wait_ge(x_loaded, 32)
            dve.wait_ge(b3_ready, 1)
            x3 = xn[:, :].rearrange("p (t f) -> p t f", f=D)
            dve.tensor_tensor(x3, x3, b3all[0:NP_, :].unsqueeze(1).to_broadcast([NP_, NT, D]), ALU.add)\
               .then_inc(xb_ready, 1)

            def add_tables(c):
                nt = chunks[c][1]
                dve.wait_ge(tab_loaded[c % 2], 16 * TABLES * (c // 2 + 1))
                wait(dve, turned, c - 1)
                dve.tensor_tensor(half[:, c % 2, 0, 0:nt * D], tab[:, c % 2, 0, 0:nt * D],
                                  tab[:, c % 2, 1, 0:nt * D], ALU.add).then_inc(half_a, 1)

            def with_bias(layer, c):
                n = chunks[c][1] * NP_
                dve.wait_ge(lin_done[layer], c + 1)
                wait(dve, hidden[layer], c - 1)
                bank = (LIN1, LIN2)[layer] + c % 2
                bias = (const_1, col_b2)[layer]
                dve.tensor_scalar(act_z[:, layer, c % 2, 0:n], ps[:, bank, 0:n], bias[:, :], None, ALU.add)\
                   .then_inc(z_ready[layer], 1)

            def softplus(layer, c):
                n = chunks[c][1] * NP_
                dve.wait_ge(log_done[layer], c + 1)
                dve.scalar_tensor_tensor(act_h[:, layer, c % 2, 0:n], act_z[:, layer, c % 2, 0:n], 0.0,
                                         act_a[:, layer, c % 2, 0:n], ALU.max, ALU.add).then_inc(hidden[layer], 1)

            def residual(c):
                t0, nt = chunks[c]
                part = xn[:, t0 * D:(t0 + nt) * D]
                dve.wait_ge(lin3_done, c + 1)
                if c == 0:
                    dve.wait_ge(xb_ready, 1)
                dve.tensor_tensor(part, part, ps[0:NP_, LIN3 + c % 2, 0:nt * D], ALU.add).then_inc(resid_done, 1)

            def statistics(c):
                t0, nt = chunks[c]
                dve.wait_ge(resid_done, c + 1)
                for t in range(nt):
                    dve.bn_stats(stats[0:NP_, c % 2, t, :], xn[:, (t0 + t) * D:(t0 + t + 1) * D])\
                       .then_inc(stats_done, 1)
                for t in range(nt):
                    dve.wait_ge(stats_done, t0 + t + 1)
                    dve.bn_aggr(mv[0:NP_, c % 2, t, :], stats[0:NP_, c % 2, t, :]).then_inc(aggr_done, 1)
                dve.wait_ge(aggr_done, t0 + nt)
                dve.tensor_scalar(var[0:NP_, c % 2, 0:nt], mv[0:NP_, c % 2, 0:nt, 1], EPS, None, ALU.add)\
                   .then_inc(var_ready, 1)

            def normalise(c):
                t0, nt = chunks[c]
                s = c % 2
                r0, v = guess[0:NP_, s, 0:nt], var[0:NP_, s, 0:nt]
                sq, br, r = (newt[0:NP_, s, j, 0:nt] for j in range(3))
                dve.wait_ge(guess_ready, c + 1)
                dve.tensor_tensor(sq, r0, r0, ALU.mult).then_inc(newt_a, 1)
                dve.wait_ge(newt_a, c + 1)
                dve.tensor_tensor(br, sq, v, ALU.mult).then_inc(newt_b, 1)
                dve.wait_ge(newt_b, c + 1)
                dve.tensor_scalar(sq, br, -0.5, 1.5, ALU.mult, ALU.add).then_inc(newt_c, 1)
                dve.wait_ge(newt_c, c + 1)
                dve.tensor_tensor(r, sq, r0, ALU.mult).then_inc(rstd_ready, 1)
                dve.wait_ge(rstd_ready, c + 1)
                for t in range(nt):
                    part = xn[:, (t0 + t) * D:(t0 + t + 1) * D]
                    last = dve.tensor_scalar(part, part, mv[0:NP_, s, t, 0:1], newt[0:NP_, s, 2, t:t + 1],
                                             ALU.subtract, ALU.mult)
                last.then_inc(normed, 1)

            for step in range(NCH + 4):
                for lag, part in enumerate((add_tables, lambda c: with_bias(0, c), lambda c: with_bias(1, c), residual)):
                    if 0 <= step - lag < NCH:
                        part(step - lag)
                if 0 <= step - 1 < NCH:
                    softplus(0, step - 1)
                if 0 <= step - 2 < NCH:
                    softplus(1, step - 2)
                if 0 <= step - 3 < NCH:
                    statistics(step - 3)
                if 0 <= step - 4 < NCH:
                    normalise(step - 4)

        @block.scalar
        def _(act):
            act.dma_start(wc[:, :, :], W_c.rearrange("(c k) m -> k c m", c=3)).then_inc(weights_loaded, 16)
            for w_sb, w in ((w1, W1), (w2, W2), (w3, W3)):
                act.dma_start(w_sb[:, :], w).then_inc(weights_loaded, 16)
            for c_sb, v in ((col_glob, glob.rearrange("a k -> (a k)")), (col_bc, b_c), (col_b1, b1), (col_b2, b2)):
                act.dma_start(c_sb[:, :], v.rearrange("(k a) -> k a", a=1)).then_inc(weights_loaded, 16)
            act.dma_start(b3row[:, :], b3.rearrange("(a k) -> a k", a=1)).then_inc(weights_loaded, 16)

            def copy_rows(i, s, quads):
                scattered_before(act, i, s)
                for q in range(quads):
                    act.wait_ge(summed, i * (SLOTS * QG) + (s * QG + q + 1))
                    act.activation(rows[:, s, q * QUAD * D:(q + 1) * QUAD * D], ps[:, SUMS + q_slot(s, q), :],
                                   ACT.Copy).then_inc(rows_ready, 1)
            over_groups(act, copy_rows)

            act.wait_ge(turned_w, 1)
            act.activation(wcT[:, :, :], ps[:, 5, 0:2 * D], ACT.Copy).then_inc(turned_w_copied, 1)
            act.wait_ge(const_c_done, 1)
            act.activation(const_c[:, :], ps[:, 6, 0:1], ACT.Identity, bias=col_bc[:, :]).then_inc(const_c_ready, 1)
            act.wait_ge(b3_spread, 1)
            act.activation(b3all[:, :], ps[:, 7, 0:D], ACT.Copy).then_inc(b3_ready, 1)
            act.wait_ge(folded, 1)
            act.activation(wxa[:, :, :], ps[:, 5, 2 * D:4 * D], ACT.Copy).then_inc(folded_ready, 1)
            act.wait_ge(const_1_done, 1)
            act.activation(const_1[:, :], ps[:, 6, 1:2], ACT.Identity, bias=col_b1[:, :]).then_inc(const_1_ready, 1)
            act.wait_ge(const_1_ready, 1)

            def copy_sums(c):
                n = chunks[c][1] * NP_
                act.wait_ge(turned, c + 1)
                wait(act, lin_done[0], c - 1)
                act.activation(aggT[:, c % 2, 0:n], ps[:, TURN + c % 2, 0:n], ACT.Copy).then_inc(aggT_ready, 1)

            def log1p_exp(layer, c):
                n = chunks[c][1] * NP_
                a = act_a[:, layer, c % 2, 0:n]
                act.wait_ge(z_ready[layer], c + 1)
                wait(act, hidden[layer], c - 1)
                act.activation(a, act_z[:, layer, c % 2, 0:n], ACT.Abs).then_inc(abs_done[layer], 1)
                act.wait_ge(abs_done[layer], c + 1)
                act.activation(a, a, ACT.Exp, scale=-1.0).then_inc(exp_done[layer], 1)
                act.wait_ge(exp_done[layer], c + 1)
                act.activation(a, a, ACT.Ln, bias=1.0).then_inc(log_done[layer], 1)

            def guess_rstd(c):
                nt = chunks[c][1]
                act.wait_ge(var_ready, c + 1)
                act.activation(logv[0:NP_, c % 2, 0:nt], var[0:NP_, c % 2, 0:nt], ACT.Ln).then_inc(logv_done, 1)
                act.wait_ge(logv_done, c + 1)
                wait(act, normed, c - 1)
                act.activation(guess[0:NP_, c % 2, 0:nt], logv[0:NP_, c % 2, 0:nt], ACT.Exp, scale=-0.5)\
                   .then_inc(guess_ready, 1)

            for step in range(NCH + 4):
                if step < NCH:
                    copy_sums(step)
                if 0 <= step - 1 < NCH:
                    log1p_exp(0, step - 1)
                if 0 <= step - 2 < NCH:
                    log1p_exp(1, step - 2)
                if 0 <= step - 4 < NCH:
                    guess_rstd(step - 4)

        @block.tensor
        def _(pe):
            def spread(i, s, q):
                if q == 0:
                    pe.wait_ge(ids_staged, i * (SLOTS * 3) + (s + 1) * 3)
                for t in range(QUAD):
                    for part in range(2):
                        mm = pe.matmul(ps[:, SPREAD + q_slot(s, q), t * P:(t + 1) * P],
                                       ids_now[:, s, part, q * QUAD + t:q * QUAD + t + 1].to_broadcast([P, P]),
                                       ident16[:, :], start=(part == 0), stop=(part == 1))
                mm.then_inc(ids_spread, 1)

            def sum_group(i, s, quads):
                last = isinstance(i, int) and i == BODIES
                pe.wait_ge(feats_loaded[s], (i + (2 if last else 1)) * 16)
                wait(pe, moved_ready, i * SLOTS + (s + 1 - SLOTS))
                for q in range(quads):
                    pe.wait_ge(same_ready, i * (SLOTS * QG) + (s * QG + q + 1))
                    wait(pe, rows_ready, i * (SLOTS * QG) + (s * QG + q - 1))
                    for t in range(QUAD):
                        j = q * QUAD + t
                        matrix = same[:, q_slot(s, q), t * P:(t + 1) * P]
                        pe.matmul(ps[:, SUMS + q_slot(s, q), t * D:(t + 1) * D], matrix,
                                  feat[:, s, j * D:(j + 1) * D], start=True, stop=True)
                        mm = pe.matmul(ps[:, COUNTS, s * GROUP + j:s * GROUP + j + 1], matrix, power,
                                       start=True, stop=True)
                    mm.then_inc(summed, 1)
                    if q + 2 < quads:
                        spread(i, s, q + 2)
                    elif not last:
                        if s + 1 < SLOTS:
                            spread(i, s + 1, q + 2 - QG)
                        else:
                            spread(i + 1, 0, q + 2 - QG)

            pe.wait_ge(ident_cast, 1)
            pe.wait_ge(spare_set, 2)
            spread(0, 0, 0)
            spread(0, 0, 1)
            over_groups(pe, sum_group)

            pe.wait_ge(weights_loaded, 16 * 9)
            pe.wait_ge(ones_set, 2)
            for part in range(2):
                mm = pe.matmul(ps[:, 5, part * D:(part + 1) * D], wc[:, part, :], ident[:, :], start=True, stop=True)
            mm.then_inc(turned_w, 1)
            pe.matmul(ps[:, 6, 0:1], wc[:, 2, :], col_glob[:, :], start=True, stop=True).then_inc(const_c_done, 1)
            pe.matmul(ps[:, 7, 0:D], ones[:, :], b3row[:, :], start=True, stop=True).then_inc(b3_spread, 1)
            pe.wait_ge(turned_w_copied, 1)
            for part in range(2):
                mm = pe.matmul(ps[:, 5, (2 + part) * D:(3 + part) * D], wcT[:, part, :], w1[:, :],
                               start=True, stop=True)
            mm.then_inc(folded, 1)
            pe.wait_ge(const_c_ready, 1)
            pe.matmul(ps[:, 6, 1:2], w1[:, :], const_c[:, :], start=True, stop=True).then_inc(const_1_done, 1)

            def turn(c):
                pe.wait_ge(half_a, c + 1)
                pe.wait_ge(half_b, c + 1)
                wait(pe, aggT_ready, c - 1)
                for t in range(chunks[c][1]):
                    for h in range(2):
                        mm = pe.matmul(ps[:, TURN + c % 2, t * NP_:(t + 1) * NP_],
                                       half[0:NP_, c % 2, h, t * D:(t + 1) * D], ident[0:NP_, 0:NP_],
                                       start=(h == 0), stop=(h == 1))
                mm.then_inc(turned, 1)

            def linear1(c):
                t0, nt = chunks[c]
                out1 = ps[:, LIN1 + c % 2, 0:nt * NP_]
                if c == 0:
                    pe.wait_ge(folded_ready, 1)
                    pe.wait_ge(const_1_ready, 1)
                    pe.wait_ge(x_loaded, 32)
                wait(pe, z_ready[0], c - 1)
                pe.matmul(out1, wxa[:, 0, :], xt[:, t0 * NP_:(t0 + nt) * NP_], start=True, stop=False)
                pe.wait_ge(aggT_ready, c + 1)
                pe.matmul(out1, wxa[:, 1, :], aggT[:, c % 2, 0:nt * NP_], start=False, stop=True)\
                  .then_inc(lin_done[0], 1)

            def linear2(c):
                n = chunks[c][1] * NP_
                pe.wait_ge(hidden[0], c + 1)
                wait(pe, z_ready[1], c - 1)
                pe.matmul(ps[:, LIN2 + c % 2, 0:n], w2[:, :], act_h[:, 0, c % 2, 0:n], start=True, stop=True)\
                  .then_inc(lin_done[1], 1)

            def linear3(c):
                pe.wait_ge(hidden[1], c + 1)
                wait(pe, resid_done, c - 1)
                for t in range(chunks[c][1]):
                    mm = pe.matmul(ps[0:NP_, LIN3 + c % 2, t * D:(t + 1) * D],
                                   act_h[:, 1, c % 2, t * NP_:(t + 1) * NP_], w3[:, :], start=True, stop=True)
                mm.then_inc(lin3_done, 1)

            for step in range(NCH + 3):
                for lag, part in enumerate((turn, linear1, linear2, linear3)):
                    if 0 <= step - lag < NCH:
                        part(step - lag)


def kernel(**inputs):
    import numpy as np
    import concourse.bacc as bacc
    from concourse import mybir as mb
    from concourse.bass_utils import run_bass_kernel_spmd

    nc = bacc.Bacc("TRN2", target_bir_lowering=False, num_devices=1)
    given = {
        "x": inputs["x"],
        "xT": np.asarray(inputs["x"]).reshape(125, 50, 128).transpose(2, 1, 0).reshape(128, 6250),
        "src": inputs["src"], "feats": inputs["edge_attr_128"],
        "glob": inputs["L0_gnn_global_feat"], "W_c": inputs["L0_gnn_W_c"], "b_c": inputs["L0_gnn_b_c"],
        "W1": inputs["L0_gnn_W1"], "b1": inputs["L0_gnn_b1"], "W2": inputs["L0_gnn_W2"],
        "b2": inputs["L0_gnn_b2"], "W3": inputs["L0_gnn_W3"], "b3": inputs["L0_gnn_b3"],
    }
    arrays, args = {}, []
    for name, a in given.items():
        a = np.ascontiguousarray(a)
        arrays[f"in_{name}"] = a
        args.append(nc.dram_tensor(f"in_{name}", a.shape, mb.dt.from_np(a.dtype), kind="ExternalInput").ap())
    args.append(nc.dram_tensor("out_rows", (6250, 128), mb.dt.float32, kind="ExternalOutput").ap())
    gnn_edge_sum_mlp_layernorm(nc, *args)
    r = run_bass_kernel_spmd(nc, [arrays], core_ids=[0])
    return r.results[0]["out_rows"]
```

```python
import concourse.bass as bass
from concourse import mybir
from contextlib import ExitStack


def gnn_edge_sum_mlp_layernorm(nc, x, xT, src, feats, glob, W_c, b_c, W1, b1, W2, b2, W3, b3, out):
    fp32, bf16, i32 = mybir.dt.float32, mybir.dt.bfloat16, mybir.dt.int32
    ALU = mybir.AluOpType
    ACT = mybir.ActivationFunctionType

    P = 128
    N, D = x.shape
    E = src.shape[0]
    COLS = E // P
    REST = E - COLS * P
    TILES = COLS + 1
    QUAD = 4
    GROUP = 8
    QG = GROUP // QUAD
    SLOTS = 4
    BODIES = TILES // (SLOTS * GROUP)
    LEFT = TILES - BODIES * SLOTS * GROUP
    TAIL = [min(GROUP, LEFT - t) // QUAD for t in range(0, LEFT, GROUP)]
    PADDED = (BODIES * SLOTS + len(TAIL)) * GROUP
    TABLES = 4
    ORDER = [0, 0, 0, 0, 1, 0, 1, 0, 1, 2, 0, 1, 2, 0, 1, 2, 3, 1, 2, 3, 1, 2, 3, 2, 3, 1, 3, 2, 3, 2, 3, 3]
    NP_ = 125
    NT = N // NP_
    ROWS = P * NT
    assert NP_ * NT == N and ROWS >= N + P and LEFT % QUAD == 0 and QG == 2 and len(TAIL) == 2
    assert len(ORDER) == SLOTS * GROUP and all(ORDER.count(k) == len(ORDER) // TABLES for k in range(TABLES))
    EPS = 1e-5

    feats_v = feats[0:COLS * P, :].rearrange("(p t) f -> p (t f)", t=COLS)
    src_v = src[0:COLS * P].rearrange("(p t) -> p t", t=COLS)
    tables = [nc.dram_tensor(f"node_table{k}", (ROWS, D), fp32, kind="Internal").ap() for k in range(TABLES)]
    tables_v = [t.rearrange("(p t) f -> p (t f)", t=NT) for t in tables]
    x_v = x.rearrange("(p t) f -> p (t f)", t=NT)
    out_v = out.rearrange("(p t) f -> p (t f)", t=NT)

    ctx = ExitStack()
    with ctx:
        def sb(name, shape, dt=fp32):
            return ctx.enter_context(nc.sbuf_tensor(name, shape, dt))

        def sem(name):
            return ctx.enter_context(nc.semaphore(name))

        ids_i = sb("ids_i", [P, PADDED], i32)
        code_i = sb("code_i", [P, PADDED], mybir.dt.uint16)
        code16 = code_i[:, :].bitcast(mybir.dt.float16)
        code_f = sb("code_f", [P, PADDED])
        to_spare = sb("to_spare", [P, PADDED])
        code_now = sb("code_now", [P, SLOTS, GROUP], mybir.dt.float16)
        feat = sb("feat", [P, SLOTS, GROUP * D])
        parts = sb("parts", [P, 2, 3, GROUP * D], bf16)
        rest = sb("rest", [P, 2, GROUP * D])
        same = sb("same", [P, 2, QUAD * P], bf16)
        rows = sb("rows", [P, SLOTS, GROUP * D])
        moved = sb("moved", [P, SLOTS, GROUP])
        index = sb("index", [P, SLOTS, GROUP], i32)
        zeros = sb("zeros", [P, 10 * D])
        ident = sb("ident", [P, P])
        ident16 = sb("ident16", [P, P], mybir.dt.float16)
        spare_i = sb("spare_i", [P, 1], i32)
        spare_f = sb("spare_f", [P, 1])
        power_i = sb("power_i", [P, 1], i32)
        power = power_i[:, :].bitcast(fp32)
        power16 = sb("power16", [P, 1], bf16)
        limit = sb("limit", [P, 1])
        wc = sb("wc", [P, 3, D])
        w1 = sb("w1", [P, D])
        w2 = sb("w2", [P, D])
        w3 = sb("w3", [P, D])
        wcT = sb("wcT", [P, 2, D])
        wxa = sb("wxa", [P, 2, D])
        col_glob = sb("col_glob", [P, 1])
        col_bc = sb("col_bc", [P, 1])
        col_b1 = sb("col_b1", [P, 1])
        col_b2 = sb("col_b2", [P, 1])
        const_c = sb("const_c", [P, 1])
        const_1 = sb("const_1", [P, 1])
        b3row = sb("b3row", [1, D])
        b3all = sb("b3all", [P, D])
        ones = sb("ones", [1, P])
        eps = sb("eps", [P, 1])
        xn = sb("xn", [NP_, NT * D])
        xt = sb("xt", [P, NT * NP_])
        CH = 4
        chunks = [(c, min(CH, NT - c)) for c in range(0, NT, CH)]
        NCH = len(chunks)
        aggT = sb("aggT", [P, 2, CH * NP_])
        act_a = sb("act_a", [P, 2, 2, CH * NP_])
        act_z = sb("act_z", [P, 2, 2, CH * NP_])
        act_h = sb("act_h", [P, 2, 2, CH * NP_])
        stats = sb("stats", [P, 2, CH, 6])
        mv = sb("mv", [P, 2, CH, 2])
        var = sb("var", [P, 2, CH])
        logv = sb("logv", [P, 2, CH])
        guess = sb("guess", [P, 2, CH])
        newt = sb("newt", [P, 2, 3, CH])
        TSLOTS = 4
        assert 2 * TABLES * CH * D == SLOTS * GROUP * D and 4 * CH * D == 2 * GROUP * D
        tab = [buf[:, 2 * h:2 * h + 2, :].rearrange("p a (k n) -> p (a k) n", k=2)
               for buf in (rows, feat) for h in range(2)]
        HSLOTS = 4
        parts_f = parts[:, :, :, :].rearrange("p s j n -> p (s j n)").bitcast(fp32)
        half = [rest[:, h, :].rearrange("p (h n) -> p h n", h=2) for h in range(2)] \
            + [parts_f[:, h * 2 * CH * D:(h + 1) * 2 * CH * D].rearrange("p (h n) -> p h n", h=2) for h in range(2)]

        ps = ctx.enter_context(nc.psum_tensor("ps", [P, 8, 512], fp32))
        SPREAD, SUMS, COUNTS = 0, 2, 4
        TURN, LIN1, LIN2, LIN3 = 0, 2, 4, 6

        zeros_set = sem("zeros_set")
        ones_set = sem("ones_set")
        pads_set = sem("pads_set")
        consts_a = sem("consts_a")
        consts_set = sem("consts_set")
        spare_set = sem("spare_set")
        ident_cast = sem("ident_cast")
        ids_loaded = sem("ids_loaded")
        codes_made = sem("codes_made")
        codes_read = sem("codes_read")
        codes_staged = sem("codes_staged")
        spare_made = sem("spare_made")
        top_ready = sem("top_ready")
        rest_ready = sem("rest_ready")
        mid_ready = sem("mid_ready")
        low_ready = sem("low_ready")
        rest_zeroed = sem("rest_zeroed")
        ids_spread = sem("ids_spread")
        same_ready = sem("same_ready")
        summed = sem("summed")
        rows_ready = sem("rows_ready")
        moved_ready = sem("moved_ready")
        index_ready = sem("index_ready")
        weights_loaded = sem("weights_loaded")
        x_loaded = sem("x_loaded")
        turned_w = sem("turned_w")
        turned_w_copied = sem("turned_w_copied")
        const_c_done = sem("const_c_done")
        const_c_ready = sem("const_c_ready")
        folded = sem("folded")
        folded_ready = sem("folded_ready")
        const_1_done = sem("const_1_done")
        const_1_ready = sem("const_1_ready")
        b3_spread = sem("b3_spread")
        b3_ready = sem("b3_ready")
        xb_ready = sem("xb_ready")
        half_ready = sem("half_ready")
        shift_ready = sem("shift_ready")
        turned = sem("turned")
        aggT_ready = sem("aggT_ready")
        lin3_done = sem("lin3_done")
        resid_done = sem("resid_done")
        stats_done = sem("stats_done")
        aggr_done = sem("aggr_done")
        var_ready = sem("var_ready")
        logv_done = sem("logv_done")
        guess_ready = sem("guess_ready")
        newt_a = sem("newt_a")
        newt_b = sem("newt_b")
        newt_c = sem("newt_c")
        rstd_ready = sem("rstd_ready")
        normed = sem("normed")
        out_sent = sem("out_sent")
        feats_loaded = [sem(f"feats_loaded{s}") for s in range(SLOTS)]
        part_zeroed = [sem(f"part_zeroed{n}") for n in range(2)]
        table_settled = [sem(f"table_settled{k}") for k in range(TABLES)]
        tab_loaded = [sem(f"tab_loaded{s}") for s in range(TSLOTS)]
        lin_done = [sem(f"lin{n}_done") for n in (1, 2)]
        abs_done = [sem(f"abs{n}_done") for n in (1, 2)]
        exp_done = [sem(f"exp{n}_done") for n in (1, 2)]
        log_done = [sem(f"log{n}_done") for n in (1, 2)]
        hidden = [sem(f"hidden{n}_ready") for n in (1, 2)]

        def wait(eng, s, value):
            if not isinstance(value, int) or value > 0:
                eng.wait_ge(s, value)

        def over_groups(eng, do):
            for i in range(2):
                for s in range(SLOTS):
                    do(i, s, QG)
            with eng.Fori(2, BODIES) as i:
                for s in range(SLOTS):
                    do(i, s, QG)
            for s, quads in enumerate(TAIL):
                do(BODIES, s, quads)

        def groups(i, s, per=1):
            return i * (SLOTS * per) + s * per

        def is_last(i, s):
            return isinstance(i, int) and (i, s) == (BODIES, len(TAIL) - 1)

        def scatters(k, i, t):
            if isinstance(i, int) and i == 0:
                return ORDER[:t].count(k)
            return i * (SLOTS * GROUP // TABLES) + (t + TABLES - 1 - k) // TABLES

        def scattered_before(eng, i, s):
            if isinstance(i, int) and i == 0:
                return
            for k in range(TABLES):
                if isinstance(i, int) and i == 1:
                    wait(eng, table_settled[k], ORDER[:(s + 1) * GROUP].count(k) * 16)
                else:
                    eng.wait_ge(table_settled[k], groups(i, s + 1 - SLOTS, GROUP // TABLES * 16))

        ZC = 10
        WRITES = NT // ZC

        def zeroed(eng, n):
            eng.wait_ge(part_zeroed[n % 2], (n // 2 + 1) * 16)

        block = ctx.enter_context(nc.Block())

        @block.sync
        def _(sp):
            sp.dma_start(ids_i[:, 0:COLS], src_v).then_inc(ids_loaded, 16)
            sp.wait_ge(pads_set, 1)
            sp.dma_start(ids_i[0:REST, COLS:TILES], src[COLS * P:E].rearrange("(p t) -> p t", t=1))\
              .then_inc(ids_loaded, 16)

            def load(i, s):
                sp.dma_start(feat[:, s, :], feats_v[:, bass.ds(groups(i, s, GROUP * D), GROUP * D)])\
                  .then_inc(feats_loaded[s], 16)

            def load_x(t):
                sp.dma_start(xn[:, bass.ds(t * D, D)], x_v[:, bass.ds(t * D, D)]).then_inc(x_loaded, 16)
                sp.dma_start(xt[:, bass.ds(t * NP_, NP_)], xT[:, bass.ds(t * NP_, NP_)]).then_inc(x_loaded, 16)

            load(0, 0)
            load(0, 1)
            sp.wait_ge(zeros_set, 1)
            for n in range(TABLES * WRITES):
                k, j = divmod(n, WRITES)
                if n >= 2:
                    zeroed(sp, n - 2)
                sp.dma_start(tables_v[k][:, j * ZC * D:(j + 1) * ZC * D], zeros[:, :])\
                  .then_inc(part_zeroed[n % 2], 16)
                if n in (0, 2):
                    load(0, 2 + n // 2)
            load_x(0)
            assert BODIES == NT
            with sp.Fori(1, BODIES) as i:
                load_x(i)
                for s in range(SLOTS):
                    sp.wait_ge(rest_ready, groups(i, s + 1 - SLOTS))
                    load(i, s)
            for s, quads in enumerate(TAIL):
                sp.wait_ge(rest_ready, groups(BODIES, s + 1 - SLOTS))
                if not is_last(BODIES, s):
                    load(BODIES, s)
            n = (TAIL[-1] * QUAD - 1) * D
            at = groups(BODIES, s, GROUP * D)
            sp.dma_start(feat[:, s, 0:n], feats_v[:, at:at + n]).then_inc(feats_loaded[s], 16)
            sp.wait_ge(rest_zeroed, 1)
            sp.dma_start(feat[0:REST, s, n:n + D], feats[COLS * P:E, :]).then_inc(feats_loaded[s], 16)

            for k in range(TABLES):
                sp.wait_ge(table_settled[k], TILES // TABLES * 16)

            STORE_LAG = 9

            def store(c):
                t0, nt = chunks[c]
                sp.wait_ge(normed, t0 + nt)
                for a, b in ((0, 112), (112, NP_)):
                    sp.dma_start(out_v[a:b, t0 * D:(t0 + nt) * D], xn[a:b, t0 * D:(t0 + nt) * D])\
                      .then_inc(out_sent, 16)

            for c, (t0, nt) in enumerate(chunks):
                wait(sp, half_ready, 2 * (c + 1 - TSLOTS))
                for k in range(TABLES):
                    sp.dma_start(tab[c % TSLOTS][:, k, 0:nt * D], tables_v[k][:, t0 * D:(t0 + nt) * D])\
                      .then_inc(tab_loaded[c % TSLOTS], 16)
                if c >= STORE_LAG:
                    store(c - STORE_LAG)
            for c in range(NCH - STORE_LAG, NCH):
                store(c)
            sp.wait_ge(out_sent, 32 * NCH)

        @block.gpsimd
        def _(pool):
            pool.iota(ids_i[:, COLS:PADDED], [[0, PADDED - COLS]], base=N, channel_multiplier=1)\
                .then_inc(pads_set, 1)
            pool.iota(spare_i[:, :], [[0, 1]], base=N, channel_multiplier=1).then_inc(consts_a, 1)
            pool.iota(power_i[:, :], [[0, 1]], base=(127 + 60) << 23, channel_multiplier=-(1 << 23))\
                .then_inc(consts_a, 1)
            pool.memset(ident[:, :], 0.0).then_inc(consts_a, 1)
            pool.wait_ge(consts_a, 3)
            pool.affine_select(out=ident[:, :], in_=ident[:, :], compare_op=ALU.not_equal, fill=1.0, base=0,
                               pattern=[[-1, P]], channel_multiplier=1).then_inc(consts_set, 1)
            def scatter(i, s, quads):
                pool.wait_ge(index_ready, groups(i, s + 1))
                for q in range(quads):
                    pool.wait_ge(rows_ready, groups(i, s, QG) + (q + 1))
                    for t in range(q * QUAD, (q + 1) * QUAD):
                        n = s * GROUP + t
                        first = isinstance(i, int) and i == 0
                        k = ORDER[n] if first else n % TABLES
                        if first and ORDER.index(k) == n:
                            zeroed(pool, (k + 1) * WRITES - 2)
                            zeroed(pool, (k + 1) * WRITES - 1)
                        wait(pool, table_settled[k], scatters(k, i, n) * 16)
                        if not isinstance(i, int):
                            pool.nop(nofuse=True)
                        pool.indirect_dma_start(
                            tables[k], bass.IndirectOffsetOnAxis(ap=index[:, s, t:t + 1], axis=0),
                            rows[:, s, t * D:(t + 1) * D], None, compute_op=ALU.add)\
                            .then_inc(table_settled[k], 16)
            over_groups(pool, scatter)

            def add_tables(c):
                nt = chunks[c][1]
                pool.wait_ge(tab_loaded[c % TSLOTS], 16 * TABLES * (c // TSLOTS + 1))
                wait(pool, turned, c + 1 - HSLOTS)
                for h in range(2):
                    pool.tensor_tensor(half[c % HSLOTS][:, h, 0:nt * D], tab[c % TSLOTS][:, 2 * h, 0:nt * D],
                                       tab[c % TSLOTS][:, 2 * h + 1, 0:nt * D], ALU.add).then_inc(half_ready, 1)

            def normalise(c):
                t0, nt = chunks[c]
                pool.wait_ge(shift_ready, c + 1)
                for t in range(nt):
                    part = xn[:, (t0 + t) * D:(t0 + t + 1) * D]
                    pool.tensor_scalar(part, part, newt[0:NP_, c % 2, 2, t:t + 1], newt[0:NP_, c % 2, 1, t:t + 1],
                                       ALU.mult, ALU.add).then_inc(normed, 1)

            for step in range(-2, NCH + 5):
                if 0 <= step + 2 < NCH:
                    add_tables(step + 2)
                if step >= 5:
                    normalise(step - 5)

        @block.vector
        def _(dve):
            dve.memset(zeros[:, :], 0.0).then_inc(zeros_set, 1)
            dve.memset(ones[:, :], 1.0).then_inc(ones_set, 1)
            dve.memset(eps[:, :], EPS).then_inc(ones_set, 1)
            dve.wait_ge(consts_a, 3)
            dve.tensor_copy(spare_f[:, :], spare_i[:, :]).then_inc(spare_set, 1)
            dve.tensor_scalar(limit[:, :], power, 2.5, None, ALU.mult).then_inc(spare_set, 1)
            dve.wait_ge(consts_set, 1)
            dve.tensor_copy(ident16[:, :], ident[:, :]).then_inc(ident_cast, 1)
            dve.tensor_copy(power16[:, :], power).then_inc(ident_cast, 1)
            dve.wait_ge(ids_loaded, 32)
            dve.tensor_scalar(code_i[:, :], ids_i[:, :], 1024.0, None, ALU.add).then_inc(codes_made, 1)

            def stage(i, s):
                dve.tensor_copy(code_now[:, s % SLOTS, :], code16[:, bass.ds(groups(i, s, GROUP), GROUP)])\
                   .then_inc(codes_staged, 1)

            dve.wait_ge(codes_made, 1)
            stage(0, 0)
            stage(0, 1)
            dve.tensor_copy(code_f[:, :], code16).then_inc(codes_read, 1)
            dve.wait_ge(spare_set, 2)
            dve.tensor_scalar(to_spare[:, :], ids_i[:, :], -1.0, spare_f[:, :], ALU.mult, ALU.add)\
               .then_inc(spare_made, 1)
            dve.wait_ge(codes_read, 1)
            dve.wait_ge(spare_made, 1)

            def split_rest(i, s, n):
                dve.wait_ge(top_ready, groups(i, s + 1))
                dve.tensor_tensor(rest[:, s % 2, 0:n], feat[:, s % SLOTS, 0:n], parts[:, s % 2, 0, 0:n],
                                  ALU.subtract).then_inc(rest_ready, 1)

            def split_low(i, s, n):
                dve.wait_ge(mid_ready, groups(i, s + 1))
                dve.tensor_tensor(parts[:, s % 2, 2, 0:n], rest[:, s % 2, 0:n], parts[:, s % 2, 1, 0:n],
                                  ALU.subtract).then_inc(low_ready, 1)

            def compare(i, s, q):
                dve.wait_ge(ids_spread, groups(i, s, QG) + (q + 1))
                dve.tensor_tensor(
                    same[:, q, :].rearrange("p (t e) -> p t e", t=QUAD),
                    ps[:, SPREAD + q, :].rearrange("p (t e) -> p t e", t=QUAD),
                    code_f[:, bass.ds(groups(i, s, GROUP) + q * QUAD, QUAD)].unsqueeze(2).to_broadcast([P, QUAD, P]),
                    ALU.is_equal).then_inc(same_ready, 1)

            def number(i, s, quads):
                n = quads * QUAD
                at = bass.ds(groups(i, s, GROUP), n)
                dve.wait_ge(summed, groups(i, s, QG) + quads)
                dve.scalar_tensor_tensor(moved[:, s, 0:n], ps[:, COUNTS, s * GROUP:s * GROUP + n], limit[:, :],
                                         to_spare[:, at], ALU.is_ge, ALU.mult).then_inc(moved_ready, 1)
                scattered_before(dve, i, s)
                dve.wait_ge(moved_ready, groups(i, s + 1))
                dve.tensor_tensor(index[:, s, 0:n], moved[:, s, 0:n], ids_i[:, at], ALU.add)\
                   .then_inc(index_ready, 1)

            def mark(i, s, quads):
                tail = isinstance(i, int) and i == BODIES
                n = (TAIL[s + 1] * QUAD if tail and s + 1 < len(TAIL) else GROUP) * D
                if tail and s == 0:
                    end = TAIL[-1] * QUAD * D
                    dve.memset(feat[:, len(TAIL) - 1, end - D:end], 0.0).then_inc(rest_zeroed, 1)
                compare(i, s, 0)
                if not tail:
                    stage(i, s + 2)
                if not is_last(i, s):
                    split_rest(i, s + 1, n)
                if quads > 1:
                    compare(i, s, 1)
                if not is_last(i, s):
                    split_low(i, s + 1, n)
                number(i, s, quads)

            split_rest(0, 0, GROUP * D)
            split_low(0, 0, GROUP * D)
            over_groups(dve, mark)

            dve.wait_ge(x_loaded, 32 * NT)
            dve.wait_ge(b3_ready, 1)
            x3 = xn[:, :].rearrange("p (t f) -> p t f", f=D)
            dve.tensor_tensor(x3, x3, b3all[0:NP_, :].unsqueeze(1).to_broadcast([NP_, NT, D]), ALU.add)\
               .then_inc(xb_ready, 1)

            def copy_sums(c):
                n = chunks[c][1] * NP_
                dve.wait_ge(turned, c + 1)
                wait(dve, lin_done[0], c - 1)
                dve.tensor_copy(aggT[:, c % 2, 0:n], ps[:, TURN + c % 2, 0:n]).then_inc(aggT_ready, 1)

            def softplus(layer, c):
                n = chunks[c][1] * NP_
                dve.wait_ge(log_done[layer], c + 1)
                dve.scalar_tensor_tensor(act_h[:, layer, c % 2, 0:n], act_z[:, layer, c % 2, 0:n], 0.0,
                                         act_a[:, layer, c % 2, 0:n], ALU.max, ALU.add).then_inc(hidden[layer], 1)

            def residual(c):
                t0, nt = chunks[c]
                part = xn[:, t0 * D:(t0 + nt) * D]
                dve.wait_ge(lin3_done, c + 1)
                if c == 0:
                    dve.wait_ge(xb_ready, 1)
                dve.tensor_tensor(part, part, ps[0:NP_, LIN3 + c % 2, 0:nt * D], ALU.add).then_inc(resid_done, 1)

            def statistics(c):
                t0, nt = chunks[c]
                dve.wait_ge(resid_done, c + 1)
                for t in range(nt):
                    dve.bn_stats(stats[0:NP_, c % 2, t, :], xn[:, (t0 + t) * D:(t0 + t + 1) * D])\
                       .then_inc(stats_done, 1)
                for t in range(nt):
                    dve.wait_ge(stats_done, t0 + t + 1)
                    dve.bn_aggr(mv[0:NP_, c % 2, t, :], stats[0:NP_, c % 2, t, :]).then_inc(aggr_done, 1)
                dve.wait_ge(aggr_done, t0 + nt)
                dve.tensor_scalar(var[0:NP_, c % 2, 0:nt], mv[0:NP_, c % 2, 0:nt, 1], EPS, None, ALU.add)\
                   .then_inc(var_ready, 1)

            def rstd(c):
                t0, nt = chunks[c]
                s = c % 2
                r0, v = guess[0:NP_, s, 0:nt], var[0:NP_, s, 0:nt]
                sq, br, r = (newt[0:NP_, s, j, 0:nt] for j in range(3))
                dve.wait_ge(guess_ready, c + 1)
                if c >= 2:
                    dve.wait_ge(normed, sum(n for _, n in chunks[:c - 1]))
                dve.tensor_tensor(sq, r0, r0, ALU.mult).then_inc(newt_a, 1)
                dve.wait_ge(newt_a, c + 1)
                dve.tensor_tensor(br, sq, v, ALU.mult).then_inc(newt_b, 1)
                dve.wait_ge(newt_b, c + 1)
                dve.tensor_scalar(sq, br, -0.5, 1.5, ALU.mult, ALU.add).then_inc(newt_c, 1)
                dve.wait_ge(newt_c, c + 1)
                dve.tensor_tensor(r, sq, r0, ALU.mult).then_inc(rstd_ready, 1)
                dve.wait_ge(rstd_ready, c + 1)
                dve.scalar_tensor_tensor(br, mv[0:NP_, s, 0:nt, 0], -1.0, r, ALU.mult, ALU.mult)\
                   .then_inc(shift_ready, 1)

            for step in range(NCH + 4):
                for lag, part in ((0, copy_sums), (3, residual), (1, lambda c: softplus(0, c)), (3, statistics),
                                  (2, lambda c: softplus(1, c)), (4, rstd)):
                    if 0 <= step - lag < NCH:
                        part(step - lag)

        @block.scalar
        def _(act):
            act.preload_act_table_set("natural_log_exp_and_others")
            act.dma_start(wc[:, :, :], W_c.rearrange("(c k) m -> k c m", c=3)).then_inc(weights_loaded, 16)
            for w_sb, w in ((w1, W1), (w2, W2), (w3, W3)):
                act.dma_start(w_sb[:, :], w).then_inc(weights_loaded, 16)
            for c_sb, v in ((col_glob, glob.rearrange("a k -> (a k)")), (col_bc, b_c), (col_b1, b1), (col_b2, b2)):
                act.dma_start(c_sb[:, :], v.rearrange("(k a) -> k a", a=1)).then_inc(weights_loaded, 16)
            act.dma_start(b3row[:, :], b3.rearrange("(a k) -> a k", a=1)).then_inc(weights_loaded, 16)

            def split_top(i, s, n):
                act.wait_ge(feats_loaded[s % SLOTS], (i + s // SLOTS) * 16 + (32 if is_last(i, s) else 16))
                wait(act, summed, groups(i, s - 1, QG))
                act.activation(parts[:, s % 2, 0, 0:n], feat[:, s % SLOTS, 0:n], ACT.Copy).then_inc(top_ready, 1)

            def split_mid(i, s, n):
                act.wait_ge(rest_ready, groups(i, s + 1))
                act.activation(parts[:, s % 2, 1, 0:n], rest[:, s % 2, 0:n], ACT.Copy).then_inc(mid_ready, 1)

            def copy_rows(i, s, q):
                act.wait_ge(summed, groups(i, s, QG) + (q + 1))
                act.activation(rows[:, s, q * QUAD * D:(q + 1) * QUAD * D], ps[:, SUMS + q, :],
                               ACT.Copy).then_inc(rows_ready, 1)

            def move(i, s, quads):
                tail = isinstance(i, int) and i == BODIES
                n = (TAIL[s + 1] * QUAD if tail and s + 1 < len(TAIL) else GROUP) * D
                if not is_last(i, s):
                    split_top(i, s + 1, n)
                scattered_before(act, i, s)
                copy_rows(i, s, 0)
                if not is_last(i, s):
                    split_mid(i, s + 1, n)
                if quads > 1:
                    copy_rows(i, s, 1)

            split_top(0, 0, GROUP * D)
            split_mid(0, 0, GROUP * D)
            over_groups(act, move)

            act.wait_ge(turned_w, 1)
            act.activation(wcT[:, :, :], ps[:, 5, 0:2 * D], ACT.Copy).then_inc(turned_w_copied, 1)
            act.wait_ge(const_c_done, 1)
            act.activation(const_c[:, :], ps[:, 6, 0:1], ACT.Identity, bias=col_bc[:, :]).then_inc(const_c_ready, 1)
            act.wait_ge(b3_spread, 1)
            act.activation(b3all[:, :], ps[:, 7, 0:D], ACT.Copy).then_inc(b3_ready, 1)
            act.wait_ge(folded, 1)
            act.activation(wxa[:, :, :], ps[:, 5, 2 * D:4 * D], ACT.Copy).then_inc(folded_ready, 1)
            act.wait_ge(const_1_done, 1)
            act.activation(const_1[:, :], ps[:, 6, 1:2], ACT.Identity, bias=col_b1[:, :]).then_inc(const_1_ready, 1)
            act.wait_ge(const_1_ready, 1)

            def log1p_exp(layer, c):
                n = chunks[c][1] * NP_
                a = act_a[:, layer, c % 2, 0:n]
                act.wait_ge(lin_done[layer], c + 1)
                wait(act, hidden[layer], c - 1)
                z = ps[:, (LIN1, LIN2)[layer] + c % 2, 0:n]
                bias = (const_1, col_b2)[layer]
                act.activation(act_z[:, layer, c % 2, 0:n], z, ACT.Identity, bias=bias[:, :])
                act.activation(a, z, ACT.Abs, bias=bias[:, :]).then_inc(abs_done[layer], 1)
                act.wait_ge(abs_done[layer], c + 1)
                act.activation(a, a, ACT.Exp, scale=-1.0).then_inc(exp_done[layer], 1)
                act.wait_ge(exp_done[layer], c + 1)
                act.activation(a, a, ACT.Ln, bias=1.0).then_inc(log_done[layer], 1)

            def guess_rstd(c):
                nt = chunks[c][1]
                act.wait_ge(var_ready, c + 1)
                act.activation(logv[0:NP_, c % 2, 0:nt], var[0:NP_, c % 2, 0:nt], ACT.Ln).then_inc(logv_done, 1)
                act.wait_ge(logv_done, c + 1)
                wait(act, shift_ready, c - 1)
                act.activation(guess[0:NP_, c % 2, 0:nt], logv[0:NP_, c % 2, 0:nt], ACT.Exp, scale=-0.5)\
                   .then_inc(guess_ready, 1)

            for step in range(NCH + 4):
                if 0 <= step - 1 < NCH:
                    log1p_exp(0, step - 1)
                if 0 <= step - 2 < NCH:
                    log1p_exp(1, step - 2)
                if 0 <= step - 4 < NCH:
                    guess_rstd(step - 4)

        @block.tensor
        def _(pe):
            def spread(i, s, q):
                if q == 0:
                    pe.wait_ge(codes_staged, groups(i, s + 1))
                for t in range(QUAD):
                    mm = pe.matmul(ps[:, SPREAD + q, t * P:(t + 1) * P],
                                   code_now[:, s % SLOTS, q * QUAD + t:q * QUAD + t + 1].to_broadcast([P, P]),
                                   ident16[:, :], start=True, stop=True)
                mm.then_inc(ids_spread, 1)

            def sum_group(i, s, quads):
                pe.wait_ge(low_ready, groups(i, s + 1))
                for q in range(quads):
                    pe.wait_ge(same_ready, groups(i, s, QG) + (q + 1))
                    wait(pe, rows_ready, groups(i, s - 1, QG) + (q + 1))
                    for t in range(QUAD):
                        j = q * QUAD + t
                        matrix = same[:, q, t * P:(t + 1) * P]
                        for part in range(3):
                            pe.matmul(ps[:, SUMS + q, t * D:(t + 1) * D], matrix,
                                      parts[:, s % 2, part, j * D:(j + 1) * D], start=(part == 0), stop=(part == 2))
                        mm = pe.matmul(ps[:, COUNTS, s * GROUP + j:s * GROUP + j + 1], matrix, power16[:, :],
                                       start=True, stop=True)
                    mm.then_inc(summed, 1)
                    if not is_last(i, s) and not (isinstance(i, int) and i == BODIES and q >= TAIL[s + 1]):
                        spread(i, s + 1, q)

            pe.wait_ge(ident_cast, 2)
            for q in range(QG):
                spread(0, 0, q)
            over_groups(pe, sum_group)

            pe.wait_ge(weights_loaded, 16 * 9)
            pe.wait_ge(ones_set, 2)
            for part in range(2):
                mm = pe.matmul(ps[:, 5, part * D:(part + 1) * D], wc[:, part, :], ident[:, :], start=True, stop=True)
            mm.then_inc(turned_w, 1)
            pe.matmul(ps[:, 6, 0:1], wc[:, 2, :], col_glob[:, :], start=True, stop=True).then_inc(const_c_done, 1)
            pe.matmul(ps[:, 7, 0:D], ones[:, :], b3row[:, :], start=True, stop=True).then_inc(b3_spread, 1)
            pe.wait_ge(turned_w_copied, 1)
            for part in range(2):
                mm = pe.matmul(ps[:, 5, (2 + part) * D:(3 + part) * D], wcT[:, part, :], w1[:, :],
                               start=True, stop=True)
            mm.then_inc(folded, 1)
            pe.wait_ge(const_c_ready, 1)
            pe.matmul(ps[:, 6, 1:2], w1[:, :], const_c[:, :], start=True, stop=True).then_inc(const_1_done, 1)

            def turn(c):
                pe.wait_ge(half_ready, 2 * (c + 1))
                wait(pe, aggT_ready, c - 1)
                for t in range(chunks[c][1]):
                    for h in range(2):
                        mm = pe.matmul(ps[:, TURN + c % 2, t * NP_:(t + 1) * NP_],
                                       half[c % HSLOTS][0:NP_, h, t * D:(t + 1) * D], ident[0:NP_, 0:NP_],
                                       start=(h == 0), stop=(h == 1))
                mm.then_inc(turned, 1)

            def linear1(c):
                t0, nt = chunks[c]
                out1 = ps[:, LIN1 + c % 2, 0:nt * NP_]
                if c == 0:
                    pe.wait_ge(folded_ready, 1)
                    pe.wait_ge(const_1_ready, 1)
                    pe.wait_ge(x_loaded, 32 * NT)
                wait(pe, abs_done[0], c - 1)
                pe.matmul(out1, wxa[:, 0, :], xt[:, t0 * NP_:(t0 + nt) * NP_], start=True, stop=False)
                pe.wait_ge(aggT_ready, c + 1)
                pe.matmul(out1, wxa[:, 1, :], aggT[:, c % 2, 0:nt * NP_], start=False, stop=True)\
                  .then_inc(lin_done[0], 1)

            def linear2(c):
                n = chunks[c][1] * NP_
                pe.wait_ge(hidden[0], c + 1)
                wait(pe, abs_done[1], c - 1)
                pe.matmul(ps[:, LIN2 + c % 2, 0:n], w2[:, :], act_h[:, 0, c % 2, 0:n], start=True, stop=True)\
                  .then_inc(lin_done[1], 1)

            def linear3(c):
                pe.wait_ge(hidden[1], c + 1)
                wait(pe, resid_done, c - 1)
                for t in range(chunks[c][1]):
                    mm = pe.matmul(ps[0:NP_, LIN3 + c % 2, t * D:(t + 1) * D],
                                   act_h[:, 1, c % 2, t * NP_:(t + 1) * NP_], w3[:, :], start=True, stop=True)
                mm.then_inc(lin3_done, 1)

            for step in range(NCH + 3):
                for lag, part in enumerate((turn, linear1, linear2, linear3)):
                    if 0 <= step - lag < NCH:
                        part(step - lag)


def kernel(**inputs):
    import numpy as np
    import concourse.bacc as bacc
    from concourse import mybir as mb
    from concourse.bass_utils import run_bass_kernel_spmd

    nc = bacc.Bacc("TRN2", target_bir_lowering=False, num_devices=1)
    given = {
        "x": inputs["x"],
        "xT": np.asarray(inputs["x"]).reshape(125, 50, 128).transpose(2, 1, 0).reshape(128, 6250),
        "src": inputs["src"], "feats": inputs["edge_attr_128"],
        "glob": inputs["L0_gnn_global_feat"], "W_c": inputs["L0_gnn_W_c"], "b_c": inputs["L0_gnn_b_c"],
        "W1": inputs["L0_gnn_W1"], "b1": inputs["L0_gnn_b1"], "W2": inputs["L0_gnn_W2"],
        "b2": inputs["L0_gnn_b2"], "W3": inputs["L0_gnn_W3"], "b3": inputs["L0_gnn_b3"],
    }
    arrays, args = {}, []
    for name, a in given.items():
        a = np.ascontiguousarray(a)
        arrays[f"in_{name}"] = a
        args.append(nc.dram_tensor(f"in_{name}", a.shape, mb.dt.from_np(a.dtype), kind="ExternalInput").ap())
    args.append(nc.dram_tensor("out_rows", (6250, 128), mb.dt.float32, kind="ExternalOutput").ap())
    gnn_edge_sum_mlp_layernorm(nc, *args)
    r = run_bass_kernel_spmd(nc, [arrays], core_ids=[0])
    return r.results[0]["out_rows"]
```

```python
import concourse.bass as bass
from concourse import mybir
from contextlib import ExitStack


def gnn_edge_sum_mlp_layernorm(nc, x, xT, src, feats, glob, W_c, b_c, W1, b1, W2, b2, W3, b3, out):
    fp32, bf16, i32 = mybir.dt.float32, mybir.dt.bfloat16, mybir.dt.int32
    ALU = mybir.AluOpType
    ACT = mybir.ActivationFunctionType

    P = 128
    N, D = x.shape
    E = src.shape[0]
    COLS = E // P
    REST = E - COLS * P
    TILES = COLS + 1
    QUAD = 4
    GROUP = 8
    QG = GROUP // QUAD
    SLOTS = 4
    BATCHES = 4
    SPANS = 11
    SPAN = -(-N // (4 * SPANS)) * 2
    PIECE = 3
    BATCH = SPANS * PIECE
    DENSE = BATCHES * BATCH
    BLOCKS = (8, 8, 8, 9)
    NB = len(BLOCKS)
    assert sum(BLOCKS) == BATCH and DENSE < COLS and 2 * NB == SLOTS * QG
    BODIES = (TILES - DENSE) // (SLOTS * GROUP)
    LEFT = TILES - DENSE - BODIES * SLOTS * GROUP
    TAIL = [min(GROUP, LEFT - t) // QUAD for t in range(0, LEFT, GROUP)]
    AHEAD = 2
    assert BODIES == AHEAD + BATCHES * SPANS
    PADDED = DENSE + (BODIES * SLOTS + 2) * GROUP
    EARLY = {(0, 1, 0): 0, (0, 2, 0): 1, (0, 3, 0): 2}
    EARLY.update({(1, n // QG, n % QG): 3 + n for n in range(SPANS - 3)})
    TABLES = 4
    ORDER = [0, 0, 0, 0, 1, 0, 1, 0, 1, 2, 0, 1, 2, 0, 1, 2, 3, 1, 2, 3, 1, 2, 3, 2, 3, 1, 3, 2, 3, 2, 3, 3]
    NP_ = 125
    NT = N // NP_
    ROWS = P * NT
    assert NP_ * NT == N and ROWS >= N + P and LEFT % QUAD == 0 and QG == 2 and len(TAIL) >= 1
    assert len(ORDER) == SLOTS * GROUP and all(ORDER.count(k) == len(ORDER) // TABLES for k in range(TABLES))
    EPS = 1e-5

    feats_v = feats[0:COLS * P, :].rearrange("(p t) f -> p (t f)", t=COLS)
    src_v = src[0:COLS * P].rearrange("(p t) -> p t", t=COLS)
    tables = [nc.dram_tensor(f"node_table{k}", (ROWS, D), fp32, kind="Internal").ap() for k in range(TABLES)]
    tables_v = [t.rearrange("(p t) f -> p (t f)", t=NT) for t in tables]
    x_v = x.rearrange("(p t) f -> p (t f)", t=NT)
    out_v = out.rearrange("(p t) f -> p (t f)", t=NT)

    ctx = ExitStack()
    with ctx:
        def sb(name, shape, dt=fp32):
            return ctx.enter_context(nc.sbuf_tensor(name, shape, dt))

        def sem(name):
            return ctx.enter_context(nc.semaphore(name))

        ids_i = sb("ids_i", [P, PADDED], i32)
        code_i = sb("code_i", [P, PADDED], mybir.dt.uint16)
        code16 = code_i[:, :].bitcast(mybir.dt.float16)
        to_spare = sb("to_spare", [P, PADDED])
        code_now = sb("code_now", [P, SLOTS, GROUP], mybir.dt.float16)
        feat = sb("feat", [P, SLOTS, GROUP * D])
        parts = sb("parts", [P, 2, 3, GROUP * D], bf16)
        rest = sb("rest", [P, 2, GROUP * D])
        same = sb("same", [P, 2, QUAD * P], bf16)
        rows = sb("rows", [P, SLOTS, GROUP * D])
        moved = sb("moved", [P, SLOTS, GROUP])
        index = sb("index", [P, SLOTS, GROUP], i32)
        splits = sb("splits", [P, 2, 3, BATCH * D], bf16)
        dfeat = sb("dfeat", [P, PIECE * D])
        drest = sb("drest", [P, PIECE * D])
        away = sb("away", [P, 2, BATCH])
        steps = sb("steps", [P, 2 * SPAN], mybir.dt.float16)
        hot = sb("hot", [P, 2, max(BLOCKS), SPAN], bf16)
        sums = sb("sums", [P, 2 * SPANS * SPAN])
        zeros = sums[:, 0:10 * D]
        zero_tile = sb("zero_tile", [P, D])
        ident = sb("ident", [P, P])
        ident16 = sb("ident16", [P, P], mybir.dt.float16)
        spare_i = sb("spare_i", [P, 1], i32)
        spare_f = sb("spare_f", [P, 1])
        power_i = sb("power_i", [P, 1], i32)
        power = power_i[:, :].bitcast(fp32)
        power16 = sb("power16", [P, 1], bf16)
        limit = sb("limit", [P, 1])
        wc = sb("wc", [P, 3, D])
        w1 = sb("w1", [P, D])
        w2 = sb("w2", [P, D])
        w3 = sb("w3", [P, D])
        wcT = sb("wcT", [P, 2, D])
        wxa = sb("wxa", [P, 2, D])
        col_glob = sb("col_glob", [P, 1])
        col_bc = sb("col_bc", [P, 1])
        col_b1 = sb("col_b1", [P, 1])
        col_b2 = sb("col_b2", [P, 1])
        const_c = sb("const_c", [P, 1])
        const_1 = sb("const_1", [P, 1])
        b3row = sb("b3row", [1, D])
        b3all = sb("b3all", [P, D])
        ones = sb("ones", [1, P])
        eps = sb("eps", [P, 1])
        xn = sb("xn", [NP_, NT * D])
        CH = 4
        chunks = [(c, min(CH, NT - c)) for c in range(0, NT, CH)]
        NCH = len(chunks)
        aggT = sb("aggT", [P, 2, CH * NP_])
        late = splits[:, :, :, :].rearrange("p b j n -> p (b j n)").bitcast(fp32)
        xt = late[:, 0:N]
        act_a, act_z, act_h = (
            late[:, N + n * 4 * CH * NP_:N + (n + 1) * 4 * CH * NP_].rearrange("p (l s n) -> p l s n", l=2, s=2)
            for n in range(3))
        stats = sb("stats", [P, 2, CH, 6])
        mv = sb("mv", [P, 2, CH, 2])
        var = sb("var", [P, 2, CH])
        logv = sb("logv", [P, 2, CH])
        guess = sb("guess", [P, 2, CH])
        newt = sb("newt", [P, 2, 3, CH])
        TSLOTS = 4
        assert 2 * TABLES * CH * D == SLOTS * GROUP * D and 4 * CH * D == 2 * GROUP * D
        tab = [buf[:, 2 * h:2 * h + 2, :].rearrange("p a (k n) -> p (a k) n", k=2)
               for buf in (rows, feat) for h in range(2)]
        HSLOTS = 4
        parts_f = parts[:, :, :, :].rearrange("p s j n -> p (s j n)").bitcast(fp32)
        half = [rest[:, h, :].rearrange("p (h n) -> p h n", h=2) for h in range(2)] \
            + [parts_f[:, h * 2 * CH * D:(h + 1) * 2 * CH * D].rearrange("p (h n) -> p h n", h=2) for h in range(2)]

        ps = ctx.enter_context(nc.psum_tensor("ps", [P, 8, 512], fp32))
        SPREAD, SUMS, COUNTS, SPANBANK = 0, 2, (4, 7), 5
        TURN, LIN1, LIN2, LIN3 = 0, 2, 4, 6

        zeros_set = sem("zeros_set")
        ones_set = sem("ones_set")
        pads_set = sem("pads_set")
        consts_a = sem("consts_a")
        consts_set = sem("consts_set")
        spare_set = sem("spare_set")
        ident_cast = sem("ident_cast")
        ids_loaded = sem("ids_loaded")
        codes_made = sem("codes_made")
        codes_staged = sem("codes_staged")
        spare_made = sem("spare_made")
        top_ready = sem("top_ready")
        rest_ready = sem("rest_ready")
        mid_ready = sem("mid_ready")
        low_ready = sem("low_ready")
        short_loaded = sem("short_loaded")
        dfeat_loaded = sem("dfeat_loaded")
        dtop_ready = sem("dtop_ready")
        drest_ready = sem("drest_ready")
        dmid_ready = sem("dmid_ready")
        dlow_ready = sem("dlow_ready")
        steps_set = sem("steps_set")
        away_ready = sem("away_ready")
        hot_made = sem("hot_made")
        hot_free = sem("hot_free")
        flushed = sem("flushed")
        ids_spread = sem("ids_spread")
        same_ready = sem("same_ready")
        summed = sem("summed")
        rows_ready = sem("rows_ready")
        moved_ready = sem("moved_ready")
        index_ready = sem("index_ready")
        weights_loaded = sem("weights_loaded")
        x_loaded = sem("x_loaded")
        turned_w = sem("turned_w")
        turned_w_copied = sem("turned_w_copied")
        const_c_done = sem("const_c_done")
        const_c_ready = sem("const_c_ready")
        folded = sem("folded")
        folded_ready = sem("folded_ready")
        const_1_done = sem("const_1_done")
        const_1_ready = sem("const_1_ready")
        b3_spread = sem("b3_spread")
        b3_ready = sem("b3_ready")
        xb_ready = sem("xb_ready")
        half_ready = sem("half_ready")
        shift_ready = sem("shift_ready")
        turned = sem("turned")
        aggT_ready = sem("aggT_ready")
        lin3_done = sem("lin3_done")
        resid_done = sem("resid_done")
        stats_done = sem("stats_done")
        aggr_done = sem("aggr_done")
        var_ready = sem("var_ready")
        logv_done = sem("logv_done")
        guess_ready = sem("guess_ready")
        newt_a = sem("newt_a")
        newt_b = sem("newt_b")
        newt_c = sem("newt_c")
        rstd_ready = sem("rstd_ready")
        normed = sem("normed")
        out_sent = sem("out_sent")
        feats_loaded = [sem(f"feats_loaded{s}") for s in range(SLOTS)]
        part_zeroed = [sem(f"part_zeroed{n}") for n in range(2)]
        table_settled = [sem(f"table_settled{k}") for k in range(TABLES)]
        tab_loaded = [sem(f"tab_loaded{s}") for s in range(TSLOTS)]
        lin_done = [sem(f"lin{n}_done") for n in (1, 2)]
        abs_done = [sem(f"abs{n}_done") for n in (1, 2)]
        exp_done = [sem(f"exp{n}_done") for n in (1, 2)]
        log_done = [sem(f"log{n}_done") for n in (1, 2)]
        hidden = [sem(f"hidden{n}_ready") for n in (1, 2)]

        def wait(eng, s, value):
            if not isinstance(value, int) or value > 0:
                eng.wait_ge(s, value)

        def over_groups(eng, do, before_batch=lambda b: None, peel=0):
            for i in range(AHEAD):
                for s in range(SLOTS):
                    do(i, s, QG, None)
            for b in range(BATCHES):
                before_batch(b)
                for c in range(peel):
                    for s in range(SLOTS):
                        do(c + (AHEAD + b * SPANS), s, QG, (b, c))
                with eng.Fori(peel, SPANS) as c:
                    for s in range(SLOTS):
                        do(c + (AHEAD + b * SPANS), s, QG, (b, c))
            for s, quads in enumerate(TAIL):
                do(BODIES, s, quads, None)

        def pieces(i, s, q, dense):
            if dense is None:
                n = EARLY.get((i, s, q))
                return [] if n is None else [(n, 0, n)]
            b, c = dense
            return [(c + (b + 1) * SPANS, b + 1, c)] if (s, q) == (1, 0) and b + 1 < BATCHES else []

        def pieces_before(i, s, q, dense):
            if dense is not None and (s, q) == (0, 0):
                first = dense[0] == 0 and isinstance(dense[1], int) and dense[1] == 0
                return pieces(AHEAD - 1, SLOTS - 1, QG - 1, None) if first else []
            if (s, q) == (0, 0):
                return [] if i in (0, BODIES) else pieces(i - 1, SLOTS - 1, QG - 1, None)
            return pieces(i, s - (q == 0), (q - 1) % QG, dense)

        def groups(i, s, per=1):
            return i * (SLOTS * per) + s * per

        def is_last(i, s):
            return isinstance(i, int) and (i, s) == (BODIES, len(TAIL) - 1)

        def scatters(k, i, t):
            if isinstance(i, int) and i == 0:
                return ORDER[:t].count(k)
            return i * (SLOTS * GROUP // TABLES) + (t + TABLES - 1 - k) // TABLES

        def scattered_before(eng, i, s):
            if isinstance(i, int) and i == 0:
                return
            for k in range(TABLES):
                if isinstance(i, int) and i == 1:
                    wait(eng, table_settled[k], ORDER[:(s + 1) * GROUP].count(k) * 16)
                else:
                    eng.wait_ge(table_settled[k], groups(i, s + 1 - SLOTS, GROUP // TABLES * 16))

        ZC = 10
        WRITES = NT // ZC

        def zeroed(eng, n):
            eng.wait_ge(part_zeroed[n % 2], (n // 2 + 1) * 16)

        block = ctx.enter_context(nc.Block())

        @block.sync
        def _(sp):
            sp.dma_start(ids_i[:, 0:COLS], src_v).then_inc(ids_loaded, 16)
            sp.wait_ge(pads_set, 1)
            sp.dma_start(ids_i[0:REST, COLS:TILES], src[COLS * P:E].rearrange("(p t) -> p t", t=1))\
              .then_inc(ids_loaded, 16)

            def load(i, s):
                sp.dma_start(feat[:, s, :], feats_v[:, bass.ds(groups(i, s, GROUP * D) + DENSE * D, GROUP * D)])\
                  .then_inc(feats_loaded[s], 16)

            def load_piece(n):
                wait(sp, drest_ready, n)
                sp.dma_start(dfeat[:, :], feats_v[:, bass.ds(n * (PIECE * D), PIECE * D)])\
                  .then_inc(dfeat_loaded, 16)

            def load_x(t):
                sp.dma_start(xn[:, bass.ds(t * D, D)], x_v[:, bass.ds(t * D, D)]).then_inc(x_loaded, 16)

            def load_next(i, s):
                sp.wait_ge(rest_ready, groups(i, s + 1 - SLOTS))
                load(i, s)

            load(0, 0)
            load(0, 1)
            between = {0: lambda: load(0, 2), 2: lambda: load(0, 3), 4: lambda: load_piece(0),
                       7: lambda: load_next(1, 0), 9: lambda: load_next(1, 1), 11: lambda: load_next(1, 2),
                       12: lambda: load_piece(1), 14: lambda: load_next(1, 3)}
            sp.wait_ge(zeros_set, 2)
            for n in range(TABLES * WRITES):
                k, j = divmod(n, WRITES)
                if n >= 2:
                    zeroed(sp, n - 2)
                sp.dma_start(tables_v[k][:, j * ZC * D:(j + 1) * ZC * D], zeros)\
                  .then_inc(part_zeroed[n % 2], 16)
                if n in between:
                    between[n]()

            def load_body(i, spare_time):
                for s in range(SLOTS):
                    load_next(i, s)
                    spare_time(s)

            load_piece(2)
            load_body(2, lambda s: [load_piece(n) for n in ([3] if s == 0 else [2 * s + 2, 2 * s + 3])])
            load_piece(10)
            for t in range(NT - (BODIES - 3)):
                load_x(t)
            with sp.Fori(0, (BATCHES - 1) * SPANS) as m:
                load_body(m + 3, lambda s: load_piece(m + SPANS) if s == 0 else None)
                load_x(m + (NT - (BODIES - 3)))
            with sp.Fori(3 + (BATCHES - 1) * SPANS, BODIES) as i:
                load_body(i, lambda s: None)
                load_x(i + (NT - BODIES))
            for s, quads in enumerate(TAIL):
                sp.wait_ge(rest_ready, groups(BODIES, s + 1 - SLOTS))
                if not is_last(BODIES, s):
                    load(BODIES, s)
            n = (TAIL[-1] * QUAD - 1) * D
            at = groups(BODIES, s, GROUP * D) + DENSE * D
            sp.dma_start(feat[0:REST, s, n:n + D], feats[COLS * P:E, :]).then_inc(short_loaded, 16)
            sp.dma_start(feat[REST:P, s, n:n + D], zero_tile[REST:P, :]).then_inc(short_loaded, 16)
            sp.wait_ge(short_loaded, 32)
            sp.dma_start(feat[:, s, 0:n], feats_v[:, at:at + n]).then_inc(feats_loaded[s], 16)

            for k in range(TABLES):
                sp.wait_ge(table_settled[k], (TILES - DENSE) // TABLES * 16)

            STORE_LAG = 9

            def store(c):
                t0, nt = chunks[c]
                sp.wait_ge(normed, t0 + nt)
                for a, b in ((0, 112), (112, NP_)):
                    sp.dma_start(out_v[a:b, t0 * D:(t0 + nt) * D], xn[a:b, t0 * D:(t0 + nt) * D])\
                      .then_inc(out_sent, 16)

            for c, (t0, nt) in enumerate(chunks):
                wait(sp, half_ready, 2 * (c + 1 - TSLOTS))
                for k in range(TABLES):
                    sp.dma_start(tab[c % TSLOTS][:, k, 0:nt * D], tables_v[k][:, t0 * D:(t0 + nt) * D])\
                      .then_inc(tab_loaded[c % TSLOTS], 16)
                sp.dma_start(xt[:, t0 * NP_:(t0 + nt) * NP_], xT[:, t0 * NP_:(t0 + nt) * NP_])\
                  .then_inc(tab_loaded[c % TSLOTS], 16)
                if c >= STORE_LAG:
                    store(c - STORE_LAG)
            for c in range(NCH - STORE_LAG, NCH):
                store(c)
            sp.wait_ge(out_sent, 32 * NCH)

        @block.gpsimd
        def _(pool):
            pool.iota(ids_i[:, COLS:PADDED], [[0, PADDED - COLS]], base=N, channel_multiplier=1)\
                .then_inc(pads_set, 1)
            pool.iota(spare_i[:, :], [[0, 1]], base=N, channel_multiplier=1).then_inc(consts_a, 1)
            pool.iota(power_i[:, :], [[0, 1]], base=(127 + 60) << 23, channel_multiplier=-(1 << 23))\
                .then_inc(consts_a, 1)
            pool.memset(ident[:, :], 0.0).then_inc(consts_a, 1)
            pool.iota(steps[:, :], [[1, 2 * SPAN]], base=0, channel_multiplier=0,
                      allow_small_or_imprecise_dtypes=True).then_inc(steps_set, 1)
            pool.wait_ge(consts_a, 3)
            pool.affine_select(out=ident[:, :], in_=ident[:, :], compare_op=ALU.not_equal, fill=1.0, base=0,
                               pattern=[[-1, P]], channel_multiplier=1).then_inc(consts_set, 1)
            def scatter(i, s, quads, dense):
                pool.wait_ge(index_ready, groups(i, s + 1))
                for q in range(quads):
                    pool.wait_ge(rows_ready, groups(i, s, QG) + (q + 1))
                    for t in range(q * QUAD, (q + 1) * QUAD):
                        n = s * GROUP + t
                        first = isinstance(i, int) and i == 0
                        k = ORDER[n] if first else n % TABLES
                        if first and ORDER.index(k) == n:
                            zeroed(pool, (k + 1) * WRITES - 2)
                            zeroed(pool, (k + 1) * WRITES - 1)
                        wait(pool, table_settled[k], scatters(k, i, n) * 16)
                        if not isinstance(i, int):
                            pool.nop(nofuse=True)
                        pool.indirect_dma_start(
                            tables[k], bass.IndirectOffsetOnAxis(ap=index[:, s, t:t + 1], axis=0),
                            rows[:, s, t * D:(t + 1) * D], None, compute_op=ALU.add)\
                            .then_inc(table_settled[k], 16)
            over_groups(pool, scatter)

            def add_tables(c):
                nt = chunks[c][1]
                pool.wait_ge(tab_loaded[c % TSLOTS], 16 * (TABLES + 1) * (c // TSLOTS + 1))
                wait(pool, turned, c + 1 - HSLOTS)
                for h in range(2):
                    pool.tensor_tensor(half[c % HSLOTS][:, h, 0:nt * D], tab[c % TSLOTS][:, 2 * h, 0:nt * D],
                                       tab[c % TSLOTS][:, 2 * h + 1, 0:nt * D], ALU.add).then_inc(half_ready, 1)

            def normalise(c):
                t0, nt = chunks[c]
                pool.wait_ge(shift_ready, c + 1)
                for t in range(nt):
                    part = xn[:, (t0 + t) * D:(t0 + t + 1) * D]
                    pool.tensor_scalar(part, part, newt[0:NP_, c % 2, 2, t:t + 1], newt[0:NP_, c % 2, 1, t:t + 1],
                                       ALU.mult, ALU.add).then_inc(normed, 1)

            for step in range(-2, NCH + 5):
                if 0 <= step + 2 < NCH:
                    add_tables(step + 2)
                if step >= 5:
                    normalise(step - 5)

        @block.vector
        def _(dve):
            dve.memset(zeros, 0.0).then_inc(zeros_set, 1)
            dve.memset(zero_tile[:, :], 0.0).then_inc(zeros_set, 1)
            dve.memset(ones[:, :], 1.0).then_inc(ones_set, 1)
            dve.memset(eps[:, :], EPS).then_inc(ones_set, 1)
            dve.wait_ge(consts_a, 3)
            dve.tensor_copy(spare_f[:, :], spare_i[:, :]).then_inc(spare_set, 1)
            dve.tensor_scalar(limit[:, :], power, 2.5, None, ALU.mult).then_inc(spare_set, 1)
            dve.wait_ge(consts_set, 1)
            dve.tensor_copy(ident16[:, :], ident[:, :]).then_inc(ident_cast, 1)
            dve.tensor_copy(power16[:, :], power).then_inc(ident_cast, 1)
            dve.wait_ge(ids_loaded, 32)
            dve.tensor_scalar(code_i[:, :], ids_i[:, :], 1024.0, None, ALU.add).then_inc(codes_made, 1)

            def stage(i, s):
                dve.tensor_copy(code_now[:, s % SLOTS, :], code16[:, bass.ds(groups(i, s, GROUP) + DENSE, GROUP)])\
                   .then_inc(codes_staged, 1)

            dve.wait_ge(codes_made, 1)
            stage(0, 0)
            stage(0, 1)
            dve.wait_ge(spare_set, 2)
            dve.tensor_scalar(to_spare[:, :], ids_i[:, :], -1.0, spare_f[:, :], ALU.mult, ALU.add)\
               .then_inc(spare_made, 1)
            dve.wait_ge(spare_made, 1)

            def split_rest(i, s, n):
                dve.wait_ge(top_ready, groups(i, s + 1))
                dve.tensor_tensor(rest[:, s % 2, 0:n], feat[:, s % SLOTS, 0:n], parts[:, s % 2, 0, 0:n],
                                  ALU.subtract).then_inc(rest_ready, 1)

            def split_low(i, s, n):
                dve.wait_ge(mid_ready, groups(i, s + 1))
                dve.tensor_tensor(parts[:, s % 2, 2, 0:n], rest[:, s % 2, 0:n], parts[:, s % 2, 1, 0:n],
                                  ALU.subtract).then_inc(low_ready, 1)

            def compare(i, s, q):
                dve.wait_ge(ids_spread, groups(i, s, QG) + (q + 1))
                dve.tensor_tensor(
                    same[:, q, :].rearrange("p (t e) -> p t e", t=QUAD),
                    ps[:, SPREAD + q, :].rearrange("p (t e) -> p t e", t=QUAD),
                    code16[:, bass.ds(groups(i, s, GROUP) + (DENSE + q * QUAD), QUAD)].unsqueeze(2).to_broadcast([P, QUAD, P]),
                    ALU.is_equal).then_inc(same_ready, 1)

            def number(i, s, quads):
                n = quads * QUAD
                at = bass.ds(groups(i, s, GROUP) + DENSE, n)
                dve.wait_ge(summed, groups(i, s, QG) + quads)
                dve.scalar_tensor_tensor(moved[:, s, 0:n], ps[:, COUNTS[s % 2], s * GROUP:s * GROUP + n], limit[:, :],
                                         to_spare[:, at], ALU.is_ge, ALU.mult).then_inc(moved_ready, 1)
                scattered_before(dve, i, s)
                dve.wait_ge(moved_ready, groups(i, s + 1))
                dve.tensor_tensor(index[:, s, 0:n], moved[:, s, 0:n], ids_i[:, at], ALU.add)\
                   .then_inc(index_ready, 1)

            def rest_of_piece(todo):
                for n, b, at in todo:
                    wait(dve, dlow_ready, n)
                    dve.wait_ge(dtop_ready, n + 1)
                    dve.tensor_tensor(drest[:, :], dfeat[:, :], splits[:, b % 2, 0, bass.ds(at * (PIECE * D), PIECE * D)],
                                      ALU.subtract).then_inc(drest_ready, 1)

            def low_of_piece(todo):
                for n, b, at in todo:
                    into = bass.ds(at * (PIECE * D), PIECE * D)
                    dve.wait_ge(dmid_ready, n + 1)
                    dve.tensor_tensor(splits[:, b % 2, 2, into], drest[:, :], splits[:, b % 2, 1, into],
                                      ALU.subtract).then_inc(dlow_ready, 1)

            def mark_nodes(b, c, m):
                h, k = divmod(m, NB)
                if m == 0:
                    dve.wait_ge(away_ready, c + (b * (SPANS + 1) + 1))
                dve.wait_ge(hot_free, (c + b * SPANS) * (2 * NB) + (m + 1))
                for u in range(BLOCKS[k]):
                    n = sum(BLOCKS[:k]) + u
                    last = dve.tensor_scalar(hot[:, m % 2, u, :], steps[:, h * SPAN:(h + 1) * SPAN],
                                             away[:, b % 2, n:n + 1], None, ALU.is_equal)
                last.then_inc(hot_made, 1)

            def flush(b, c, h):
                dve.wait_ge(hot_free, (c + b * SPANS) * (2 * NB) + (2 + (h + 1) * NB))
                into = sums[:, bass.ds(c * (2 * SPAN) + h * SPAN, SPAN)]
                if b == 0:
                    dve.tensor_copy(into, ps[:, SPANBANK + h, 0:SPAN]).then_inc(flushed, 1)
                else:
                    dve.tensor_tensor(into, into, ps[:, SPANBANK + h, 0:SPAN], ALU.add).then_inc(flushed, 1)

            def flush_before(b, c):
                if isinstance(c, int) and c == 0:
                    b, c = b - 1, SPANS
                if b >= 0:
                    flush(b, c - 1, 1)

            def mark(i, s, quads, dense):
                tail = isinstance(i, int) and i == BODIES
                first = isinstance(i, int) and i == 0
                n = (TAIL[s + 1] * QUAD if tail and s + 1 < len(TAIL) else GROUP) * D
                for q in range(quads):
                    compare(i, s, q)
                    if dense is not None:
                        mark_nodes(*dense, s * QG + q)
                    if q == 0 and not first and not (isinstance(i, int) and (i, s) == (1, 0)):
                        if s == 0:
                            number(i - 1, SLOTS - 1, QG)
                        else:
                            number(i, s - 1, QG)
                    if q == 0 and not tail:
                        stage(i, s + 2)
                    if not is_last(i, s):
                        (split_rest if q == 0 else split_low)(i, s + 1, n)
                    low_of_piece(pieces_before(i, s, q, dense))
                    rest_of_piece(pieces(i, s, q, dense))
                    if dense is not None and s * QG + q == 1:
                        flush_before(*dense)
                    if dense is not None and s * QG + q == NB + 1:
                        flush(*dense, 0)
                if first or is_last(i, s):
                    number(i, s, quads)
                if dense is not None and s == SLOTS - 1:
                    dve.wait_ge(hot_made, (dense[1] + dense[0] * SPANS + 1) * (2 * NB))
                    dve.tensor_scalar(away[:, dense[0] % 2, :], away[:, dense[0] % 2, :], float(-2 * SPAN), None,
                                      ALU.add).then_inc(away_ready, 1)

            def first_span(b):
                dve.tensor_copy(away[:, b % 2, :], ids_i[:, b * BATCH:(b + 1) * BATCH]).then_inc(away_ready, 1)

            split_rest(0, 0, GROUP * D)
            split_low(0, 0, GROUP * D)
            dve.wait_ge(steps_set, 1)
            over_groups(dve, mark, first_span, peel=1)
            flush(BATCHES - 1, SPANS - 1, 1)

            dve.wait_ge(x_loaded, 16 * NT)
            dve.wait_ge(b3_ready, 1)
            x3 = xn[:, :].rearrange("p (t f) -> p t f", f=D)
            dve.tensor_tensor(x3, x3, b3all[0:NP_, :].unsqueeze(1).to_broadcast([NP_, NT, D]), ALU.add)\
               .then_inc(xb_ready, 1)

            def copy_sums(c):
                n = chunks[c][1] * NP_
                dve.wait_ge(turned, c + 1)
                wait(dve, lin_done[0], c - 1)
                t0, nt = chunks[c]
                dve.tensor_tensor(aggT[:, c % 2, 0:n].rearrange("f (t p) -> f t p", p=NP_),
                                  ps[:, TURN + c % 2, 0:n].rearrange("f (t p) -> f t p", p=NP_),
                                  sums[:, 0:N].rearrange("f (p t) -> f t p", t=NT)[:, t0:t0 + nt, :],
                                  ALU.add).then_inc(aggT_ready, 1)

            def softplus(layer, c):
                n = chunks[c][1] * NP_
                dve.wait_ge(log_done[layer], c + 1)
                dve.scalar_tensor_tensor(act_h[:, layer, c % 2, 0:n], act_z[:, layer, c % 2, 0:n], 0.0,
                                         act_a[:, layer, c % 2, 0:n], ALU.max, ALU.add).then_inc(hidden[layer], 1)

            def residual(c):
                t0, nt = chunks[c]
                part = xn[:, t0 * D:(t0 + nt) * D]
                dve.wait_ge(lin3_done, c + 1)
                if c == 0:
                    dve.wait_ge(xb_ready, 1)
                dve.tensor_tensor(part, part, ps[0:NP_, LIN3 + c % 2, 0:nt * D], ALU.add).then_inc(resid_done, 1)

            def statistics(c):
                t0, nt = chunks[c]
                dve.wait_ge(resid_done, c + 1)
                for t in range(nt):
                    dve.bn_stats(stats[0:NP_, c % 2, t, :], xn[:, (t0 + t) * D:(t0 + t + 1) * D])\
                       .then_inc(stats_done, 1)
                for t in range(nt):
                    dve.wait_ge(stats_done, t0 + t + 1)
                    dve.bn_aggr(mv[0:NP_, c % 2, t, :], stats[0:NP_, c % 2, t, :]).then_inc(aggr_done, 1)
                dve.wait_ge(aggr_done, t0 + nt)
                dve.tensor_scalar(var[0:NP_, c % 2, 0:nt], mv[0:NP_, c % 2, 0:nt, 1], EPS, None, ALU.add)\
                   .then_inc(var_ready, 1)

            def rstd(c):
                t0, nt = chunks[c]
                s = c % 2
                r0, v = guess[0:NP_, s, 0:nt], var[0:NP_, s, 0:nt]
                sq, br, r = (newt[0:NP_, s, j, 0:nt] for j in range(3))
                dve.wait_ge(guess_ready, c + 1)
                if c >= 2:
                    dve.wait_ge(normed, sum(n for _, n in chunks[:c - 1]))
                dve.tensor_tensor(sq, r0, r0, ALU.mult).then_inc(newt_a, 1)
                dve.wait_ge(newt_a, c + 1)
                dve.tensor_tensor(br, sq, v, ALU.mult).then_inc(newt_b, 1)
                dve.wait_ge(newt_b, c + 1)
                dve.tensor_scalar(sq, br, -0.5, 1.5, ALU.mult, ALU.add).then_inc(newt_c, 1)
                dve.wait_ge(newt_c, c + 1)
                dve.tensor_tensor(r, sq, r0, ALU.mult).then_inc(rstd_ready, 1)
                dve.wait_ge(rstd_ready, c + 1)
                dve.scalar_tensor_tensor(br, mv[0:NP_, s, 0:nt, 0], -1.0, r, ALU.mult, ALU.mult)\
                   .then_inc(shift_ready, 1)

            for step in range(NCH + 4):
                for lag, part in ((0, copy_sums), (3, residual), (1, lambda c: softplus(0, c)), (3, statistics),
                                  (2, lambda c: softplus(1, c)), (4, rstd)):
                    if 0 <= step - lag < NCH:
                        part(step - lag)

        @block.scalar
        def _(act):
            act.preload_act_table_set("natural_log_exp_and_others")
            act.dma_start(wc[:, :, :], W_c.rearrange("(c k) m -> k c m", c=3)).then_inc(weights_loaded, 16)
            for w_sb, w in ((w1, W1), (w2, W2), (w3, W3)):
                act.dma_start(w_sb[:, :], w).then_inc(weights_loaded, 16)
            for c_sb, v in ((col_glob, glob.rearrange("a k -> (a k)")), (col_bc, b_c), (col_b1, b1), (col_b2, b2)):
                act.dma_start(c_sb[:, :], v.rearrange("(k a) -> k a", a=1)).then_inc(weights_loaded, 16)
            act.dma_start(b3row[:, :], b3.rearrange("(a k) -> a k", a=1)).then_inc(weights_loaded, 16)

            def split_top(i, s, n):
                act.wait_ge(feats_loaded[s % SLOTS], (i + s // SLOTS) * 16 + 16)
                wait(act, summed, groups(i, s - 1, QG))
                act.activation(parts[:, s % 2, 0, 0:n], feat[:, s % SLOTS, 0:n], ACT.Copy).then_inc(top_ready, 1)

            def split_mid(i, s, n):
                act.wait_ge(rest_ready, groups(i, s + 1))
                act.activation(parts[:, s % 2, 1, 0:n], rest[:, s % 2, 0:n], ACT.Copy).then_inc(mid_ready, 1)

            def copy_rows(i, s, q):
                act.wait_ge(summed, groups(i, s, QG) + (q + 1))
                act.activation(rows[:, s, q * QUAD * D:(q + 1) * QUAD * D], ps[:, SUMS + q, :],
                               ACT.Copy).then_inc(rows_ready, 1)

            def top_of_piece(todo):
                for n, b, at in todo:
                    act.wait_ge(dfeat_loaded, n * 16 + 16)
                    if b >= 2:
                        act.wait_ge(hot_free, (b - 1) * SPANS * (2 * NB) + 2)
                    act.activation(splits[:, b % 2, 0, bass.ds(at * (PIECE * D), PIECE * D)], dfeat[:, :],
                                   ACT.Copy).then_inc(dtop_ready, 1)

            def mid_of_piece(todo):
                for n, b, at in todo:
                    act.wait_ge(drest_ready, n + 1)
                    act.activation(splits[:, b % 2, 1, bass.ds(at * (PIECE * D), PIECE * D)], drest[:, :],
                                   ACT.Copy).then_inc(dmid_ready, 1)

            def move(i, s, quads, dense):
                tail = isinstance(i, int) and i == BODIES
                n = (TAIL[s + 1] * QUAD if tail and s + 1 < len(TAIL) else GROUP) * D
                if not is_last(i, s):
                    split_top(i, s + 1, n)
                top_of_piece(pieces(i, s, 0, dense))
                scattered_before(act, i, s)
                copy_rows(i, s, 0)
                if not is_last(i, s):
                    split_mid(i, s + 1, n)
                mid_of_piece(pieces(i, s, 0, dense))
                top_of_piece(pieces(i, s, 1, dense))
                if quads > 1:
                    copy_rows(i, s, 1)
                mid_of_piece(pieces(i, s, 1, dense))

            split_top(0, 0, GROUP * D)
            split_mid(0, 0, GROUP * D)
            over_groups(act, move)

            act.wait_ge(turned_w, 1)
            act.activation(wcT[:, :, :], ps[:, 5, 0:2 * D], ACT.Copy).then_inc(turned_w_copied, 1)
            act.wait_ge(const_c_done, 1)
            act.activation(const_c[:, :], ps[:, 6, 0:1], ACT.Identity, bias=col_bc[:, :]).then_inc(const_c_ready, 1)
            act.wait_ge(b3_spread, 1)
            act.activation(b3all[:, :], ps[:, 7, 0:D], ACT.Copy).then_inc(b3_ready, 1)
            act.wait_ge(folded, 1)
            act.activation(wxa[:, :, :], ps[:, 5, 2 * D:4 * D], ACT.Copy).then_inc(folded_ready, 1)
            act.wait_ge(const_1_done, 1)
            act.activation(const_1[:, :], ps[:, 6, 1:2], ACT.Identity, bias=col_b1[:, :]).then_inc(const_1_ready, 1)
            act.wait_ge(const_1_ready, 1)

            def log1p_exp(layer, c):
                n = chunks[c][1] * NP_
                a = act_a[:, layer, c % 2, 0:n]
                act.wait_ge(lin_done[layer], c + 1)
                wait(act, hidden[layer], c - 1)
                z = ps[:, (LIN1, LIN2)[layer] + c % 2, 0:n]
                bias = (const_1, col_b2)[layer]
                act.activation(act_z[:, layer, c % 2, 0:n], z, ACT.Identity, bias=bias[:, :])
                act.activation(a, z, ACT.Abs, bias=bias[:, :]).then_inc(abs_done[layer], 1)
                act.wait_ge(abs_done[layer], c + 1)
                act.activation(a, a, ACT.Exp, scale=-1.0).then_inc(exp_done[layer], 1)
                act.wait_ge(exp_done[layer], c + 1)
                act.activation(a, a, ACT.Ln, bias=1.0).then_inc(log_done[layer], 1)

            def guess_rstd(c):
                nt = chunks[c][1]
                act.wait_ge(var_ready, c + 1)
                act.activation(logv[0:NP_, c % 2, 0:nt], var[0:NP_, c % 2, 0:nt], ACT.Ln).then_inc(logv_done, 1)
                act.wait_ge(logv_done, c + 1)
                wait(act, shift_ready, c - 1)
                act.activation(guess[0:NP_, c % 2, 0:nt], logv[0:NP_, c % 2, 0:nt], ACT.Exp, scale=-0.5)\
                   .then_inc(guess_ready, 1)

            for step in range(NCH + 4):
                if 0 <= step - 1 < NCH:
                    log1p_exp(0, step - 1)
                if 0 <= step - 2 < NCH:
                    log1p_exp(1, step - 2)
                if 0 <= step - 4 < NCH:
                    guess_rstd(step - 4)

        @block.tensor
        def _(pe):
            def spread(i, s, q):
                if q == 0:
                    pe.wait_ge(codes_staged, groups(i, s + 1))
                for t in range(QUAD):
                    mm = pe.matmul(ps[:, SPREAD + q, t * P:(t + 1) * P],
                                   code_now[:, s % SLOTS, q * QUAD + t:q * QUAD + t + 1].to_broadcast([P, P]),
                                   ident16[:, :], start=True, stop=True)
                mm.then_inc(ids_spread, 1)

            def sum_nodes(b, c, m):
                h, k = divmod(m, NB)
                if m == 0:
                    pe.wait_ge(dlow_ready, (b + 1) * SPANS)
                pe.wait_ge(hot_made, (c + b * SPANS) * (2 * NB) + (m + 1))
                for u in range(BLOCKS[k]):
                    n = sum(BLOCKS[:k]) + u
                    for part in range(3):
                        mm = pe.matmul(ps[:, SPANBANK + h, 0:SPAN], splits[:, b % 2, part, n * D:(n + 1) * D],
                                       hot[:, m % 2, u, :],
                                       start=(n == 0 and part == 0), stop=(n == BATCH - 1 and part == 2))
                mm.then_inc(hot_free, 1)

            def sum_group(i, s, quads, dense):
                pe.wait_ge(low_ready, groups(i, s + 1))
                for q in range(quads):
                    pe.wait_ge(same_ready, groups(i, s, QG) + (q + 1))
                    wait(pe, rows_ready, groups(i, s - 1, QG) + (q + 1))
                    for t in range(QUAD):
                        j = q * QUAD + t
                        matrix = same[:, q, t * P:(t + 1) * P]
                        for part in range(3):
                            pe.matmul(ps[:, SUMS + q, t * D:(t + 1) * D], matrix,
                                      parts[:, s % 2, part, j * D:(j + 1) * D], start=(part == 0), stop=(part == 2))
                        mm = pe.matmul(ps[:, COUNTS[s % 2], s * GROUP + j:s * GROUP + j + 1], matrix, power16[:, :],
                                       start=True, stop=True)
                    mm.then_inc(summed, 1)
                    if not is_last(i, s) and not (isinstance(i, int) and i == BODIES and q >= TAIL[s + 1]):
                        spread(i, s + 1, q)
                    if dense is not None:
                        sum_nodes(*dense, s * QG + q)

            pe.sem_inc(hot_free, 2)
            pe.wait_ge(ident_cast, 2)
            for q in range(QG):
                spread(0, 0, q)
            over_groups(pe, sum_group)

            pe.wait_ge(weights_loaded, 16 * 9)
            pe.wait_ge(ones_set, 2)
            pe.wait_ge(flushed, 2 * SPANS * BATCHES)
            for part in range(2):
                mm = pe.matmul(ps[:, 5, part * D:(part + 1) * D], wc[:, part, :], ident[:, :], start=True, stop=True)
            mm.then_inc(turned_w, 1)
            pe.matmul(ps[:, 6, 0:1], wc[:, 2, :], col_glob[:, :], start=True, stop=True).then_inc(const_c_done, 1)
            pe.matmul(ps[:, 7, 0:D], ones[:, :], b3row[:, :], start=True, stop=True).then_inc(b3_spread, 1)
            pe.wait_ge(turned_w_copied, 1)
            for part in range(2):
                mm = pe.matmul(ps[:, 5, (2 + part) * D:(3 + part) * D], wcT[:, part, :], w1[:, :],
                               start=True, stop=True)
            mm.then_inc(folded, 1)
            pe.wait_ge(const_c_ready, 1)
            pe.matmul(ps[:, 6, 1:2], w1[:, :], const_c[:, :], start=True, stop=True).then_inc(const_1_done, 1)

            def turn(c):
                pe.wait_ge(half_ready, 2 * (c + 1))
                wait(pe, aggT_ready, c - 1)
                for t in range(chunks[c][1]):
                    for h in range(2):
                        mm = pe.matmul(ps[:, TURN + c % 2, t * NP_:(t + 1) * NP_],
                                       half[c % HSLOTS][0:NP_, h, t * D:(t + 1) * D], ident[0:NP_, 0:NP_],
                                       start=(h == 0), stop=(h == 1))
                mm.then_inc(turned, 1)

            def linear1(c):
                t0, nt = chunks[c]
                out1 = ps[:, LIN1 + c % 2, 0:nt * NP_]
                if c == 0:
                    pe.wait_ge(folded_ready, 1)
                    pe.wait_ge(const_1_ready, 1)
                wait(pe, abs_done[0], c - 1)
                pe.matmul(out1, wxa[:, 0, :], xt[:, t0 * NP_:(t0 + nt) * NP_], start=True, stop=False)
                pe.wait_ge(aggT_ready, c + 1)
                pe.matmul(out1, wxa[:, 1, :], aggT[:, c % 2, 0:nt * NP_], start=False, stop=True)\
                  .then_inc(lin_done[0], 1)

            def linear2(c):
                n = chunks[c][1] * NP_
                pe.wait_ge(hidden[0], c + 1)
                wait(pe, abs_done[1], c - 1)
                pe.matmul(ps[:, LIN2 + c % 2, 0:n], w2[:, :], act_h[:, 0, c % 2, 0:n], start=True, stop=True)\
                  .then_inc(lin_done[1], 1)

            def linear3(c):
                pe.wait_ge(hidden[1], c + 1)
                wait(pe, resid_done, c - 1)
                for t in range(chunks[c][1]):
                    mm = pe.matmul(ps[0:NP_, LIN3 + c % 2, t * D:(t + 1) * D],
                                   act_h[:, 1, c % 2, t * NP_:(t + 1) * NP_], w3[:, :], start=True, stop=True)
                mm.then_inc(lin3_done, 1)

            for step in range(NCH + 3):
                for lag, part in enumerate((turn, linear1, linear2, linear3)):
                    if 0 <= step - lag < NCH:
                        part(step - lag)


def kernel(**inputs):
    import numpy as np
    import concourse.bacc as bacc
    from concourse import mybir as mb
    from concourse.bass_utils import run_bass_kernel_spmd

    nc = bacc.Bacc("TRN2", target_bir_lowering=False, num_devices=1)
    given = {
        "x": inputs["x"],
        "xT": np.asarray(inputs["x"]).reshape(125, 50, 128).transpose(2, 1, 0).reshape(128, 6250),
        "src": inputs["src"], "feats": inputs["edge_attr_128"],
        "glob": inputs["L0_gnn_global_feat"], "W_c": inputs["L0_gnn_W_c"], "b_c": inputs["L0_gnn_b_c"],
        "W1": inputs["L0_gnn_W1"], "b1": inputs["L0_gnn_b1"], "W2": inputs["L0_gnn_W2"],
        "b2": inputs["L0_gnn_b2"], "W3": inputs["L0_gnn_W3"], "b3": inputs["L0_gnn_b3"],
    }
    arrays, args = {}, []
    for name, a in given.items():
        a = np.ascontiguousarray(a)
        arrays[f"in_{name}"] = a
        args.append(nc.dram_tensor(f"in_{name}", a.shape, mb.dt.from_np(a.dtype), kind="ExternalInput").ap())
    args.append(nc.dram_tensor("out_rows", (6250, 128), mb.dt.float32, kind="ExternalOutput").ap())
    gnn_edge_sum_mlp_layernorm(nc, *args)
    r = run_bass_kernel_spmd(nc, [arrays], core_ids=[0])
    return r.results[0]["out_rows"]
```
